# Optimizing a Trainium2 kernel written in Bass

```python
import numpy as np
import jax
import jax.numpy as jnp

def _softmax(x, axis=-1):
    return jax.nn.softmax(x, axis=axis)

def _gelu(x):
    return jax.nn.gelu(x, approximate=True)

def _silu(x):
    return jax.nn.silu(x)

def _sigmoid(x):
    return jax.nn.sigmoid(x)

def _layernorm(x, axis=-1, eps=1e-05):
    m = jnp.mean(x, axis=axis, keepdims=True)
    v = jnp.var(x, axis=axis, keepdims=True)
    return (x - m) / jnp.sqrt(v + eps)

def _scatter_add(tgt, idx, src, axis=0):
    return tgt.at[idx].add(src)

def _segment_sum(src, seg, n):
    return jax.ops.segment_sum(src, seg, n)
kernel_name = 'mk_cond_resid_d2_seqx_r8_415984'

def setup_inputs(seed: int=0):
    np.random.seed(seed)
    _w = jnp.asarray

    def _rec_inputs():
        import jax
        import jax.numpy as jnp
        _rk = jax.random.key(seed)
        x = -1.394e-06 + 0.9999 * jax.random.normal(jax.random.fold_in(_rk, 1), (32, 32, 256), jnp.float32)
        _lenS = 32 - jax.random.randint(jax.random.fold_in(_rk, 7), (32,), 0, max(1, 32 // 4) + 1, jnp.int32)
        _lenS2 = 32 - jax.random.randint(jax.random.fold_in(_rk, 8), (32,), 0, max(1, 32 // 4) + 1, jnp.int32)
        cond_2048 = -0.00499425 + 1.0058 * jax.random.normal(jax.random.fold_in(_rk, 11), (32, 256), jnp.float32)
        return (x, cond_2048)
    x, cond_2048 = _rec_inputs()

    def _L0_cond_setup():
        import jax, jax.numpy as jnp
        import numpy as np
        B, T, D = (16, 128, 256)
        key = jax.random.key(seed)
        k0, k1, k2, k3 = jax.random.split(key, 4)
        scale = 1.0 / np.sqrt(D)
        return {'initial_state': jax.random.normal(k0, (B, D), jnp.float32), 'inputs': jax.random.normal(k1, (B, T, D), jnp.float32), 'W_ih': jax.random.normal(k2, (D, 3 * D), jnp.float32) * scale, 'W_hh': jax.random.normal(k3, (D, 3 * D), jnp.float32) * scale, 'b_ih': jnp.zeros((3 * D,), jnp.float32), 'b_hh': jnp.zeros((3 * D,), jnp.float32)}
    _L0_cond_all = _L0_cond_setup()
    _L0_cond_in = {k: v for k, v in _L0_cond_all.items() if k in ('W_ih', 'W_hh', 'b_ih', 'b_hh')}
    del _L0_cond_all

    def _L1_cond_setup():
        import jax, jax.numpy as jnp
        import numpy as np
        HEADS = 16
        EPS = 1e-06

        def _rms_norm(x, g):
            xf = x.astype(jnp.float32)
            y = xf * jax.lax.rsqrt(jnp.mean(xf * xf, axis=-1, keepdims=True) + EPS)
            return y.astype(x.dtype) * g
        key = jax.random.key(seed)
        ks = jax.random.split(key, 6)
        b, n, dim, emb_dim = (4, 256, 256, 256)
        d_head = dim // HEADS
        return {'x': jax.random.normal(ks[0], (b, n, dim), jnp.float32), 'emb': jax.random.normal(ks[1], (b, 1, emb_dim), jnp.float32), 'W_emb': jax.random.normal(ks[2], (emb_dim, 2 * dim), jnp.float32) * emb_dim ** (-0.5), 'b_emb': jnp.zeros((2 * dim,), jnp.float32), 'g_norm': jnp.ones((dim,), jnp.float32), 'W_qkv': jax.random.normal(ks[3], (dim, 3 * dim), jnp.float32) * dim ** (-0.5), 'g_q': jnp.ones((d_head,), jnp.float32), 'g_k': jnp.ones((d_head,), jnp.float32), 'W_out': jax.random.normal(ks[4], (dim, dim), jnp.float32) * dim ** (-0.5)}
    _L1_cond_all = _L1_cond_setup()
    _L1_cond_in = {k: v for k, v in _L1_cond_all.items() if k in ('W_emb', 'b_emb', 'g_norm', 'W_qkv', 'g_q', 'g_k', 'W_out')}
    del _L1_cond_all
    return {'x': x, 'cond_2048': cond_2048, 'L0_cond_W_ih': _L0_cond_in['W_ih'], 'L0_cond_W_hh': _L0_cond_in['W_hh'], 'L0_cond_b_ih': _L0_cond_in['b_ih'], 'L0_cond_b_hh': _L0_cond_in['b_hh'], 'L1_cond_W_emb': _L1_cond_in['W_emb'], 'L1_cond_b_emb': _L1_cond_in['b_emb'], 'L1_cond_g_norm': _L1_cond_in['g_norm'], 'L1_cond_W_qkv': _L1_cond_in['W_qkv'], 'L1_cond_g_q': _L1_cond_in['g_q'], 'L1_cond_g_k': _L1_cond_in['g_k'], 'L1_cond_W_out': _L1_cond_in['W_out']}

def reference(x, cond_2048, L0_cond_W_ih, L0_cond_W_hh, L0_cond_b_ih, L0_cond_b_hh, L1_cond_W_emb, L1_cond_b_emb, L1_cond_g_norm, L1_cond_W_qkv, L1_cond_g_q, L1_cond_g_k, L1_cond_W_out):
    import jax
    import jax.numpy as jnp

    def _L0_cond_ref(initial_state, inputs, W_ih, W_hh, b_ih, b_hh):
        import jax, jax.numpy as jnp
        import numpy as np
        B, T, D = (16, 128, 256)
        "ScanOverTime(GRU cell): sequential per-timestep module call with\n            dict-state passing; merge_dict_trees stacks the per-step\n            'state_predicted' tensors along axis=1 -> [B, T, D]."

        def cell(h, x):
            gi = x @ W_ih + b_ih
            gh = h @ W_hh + b_hh
            i_r, i_z, i_n = jnp.split(gi, 3, axis=-1)
            h_r, h_z, h_n = jnp.split(gh, 3, axis=-1)
            r = jax.nn.sigmoid(i_r + h_r)
            z = jax.nn.sigmoid(i_z + h_z)
            n = jnp.tanh(i_n + r * h_n)
            h_new = (1.0 - z) * n + z * h
            return (h_new, h_new)
        xs = jnp.swapaxes(inputs, 0, 1)
        _, hs = jax.lax.scan(cell, initial_state, xs)
        return jnp.swapaxes(hs, 0, 1)

    def _L1_cond_ref(x, emb, W_emb, b_emb, g_norm, W_qkv, g_q, g_k, W_out):
        import jax, jax.numpy as jnp
        import numpy as np
        HEADS = 16
        EPS = 1e-06

        def _rms_norm(x, g):
            xf = x.astype(jnp.float32)
            y = xf * jax.lax.rsqrt(jnp.mean(xf * xf, axis=-1, keepdims=True) + EPS)
            return y.astype(x.dtype) * g
        b, n, dim = x.shape
        h = HEADS
        d = dim // h
        scale_shift = emb @ W_emb + b_emb
        scale, shift = jnp.split(scale_shift, 2, axis=-1)
        xn = _rms_norm(x, g_norm) * (1.0 + scale) + shift
        qkv = xn @ W_qkv
        qkv = qkv.reshape(b, n, 3, h, d)
        q, k, v = jnp.moveaxis(qkv, 2, 0)
        q = jnp.swapaxes(q, 1, 2)
        k = jnp.swapaxes(k, 1, 2)
        v = jnp.swapaxes(v, 1, 2)
        q = _rms_norm(q, g_q)
        k = _rms_norm(k, g_k)
        logits = jnp.einsum('bhqd,bhkd->bhqk', q, k) * d ** (-0.5)
        attn = jax.nn.softmax(logits, axis=-1)
        o = jnp.einsum('bhqk,bhkd->bhqd', attn, v)
        o = jnp.swapaxes(o, 1, 2).reshape(b, n, dim)
        return o + o @ W_out
    x = x + _L0_cond_ref(cond_2048, x, L0_cond_W_ih, L0_cond_W_hh, L0_cond_b_ih, L0_cond_b_hh)
    x = x + _L1_cond_ref(x, cond_2048[:, None, :], L1_cond_W_emb, L1_cond_b_emb, L1_cond_g_norm, L1_cond_W_qkv, L1_cond_g_q, L1_cond_g_k, L1_cond_W_out)
    return x

_drawn_inputs = setup_inputs


def setup_inputs(seed=0):
    import zlib

    import numpy as np

    out = dict(_drawn_inputs(seed))
    spreads = {'L0_cond_b_ih': (0.0, 0.1),
     'L0_cond_b_hh': (0.0, 0.1),
     'L1_cond_b_emb': (0.0, 0.1),
     'L1_cond_g_norm': (1.0, 0.2),
     'L1_cond_g_q': (1.0, 0.2),
     'L1_cond_g_k': (1.0, 0.582)}
    factors = {}
    for name, (base, spread) in spreads.items():
        noise = np.random.default_rng([zlib.crc32(name.encode()), seed]).standard_normal(out[name].shape)
        drawn = base * np.exp(spread * noise) if base else spread * noise
        out[name] = jnp.asarray(drawn.astype(out[name].dtype))
    for name, factor in factors.items():
        out[name] = (out[name] * factor).astype(out[name].dtype)
    return out
```

```python
from contextlib import ExitStack

import concourse.bass as bass
from concourse import mybir

F32 = mybir.dt.float32
BF16 = mybir.dt.bfloat16
ALU = mybir.AluOpType
ACT = mybir.ActivationFunctionType
AX = mybir.AxisListType

P = 128
B, T, D = 32, 32, 256
J = 4
C = D // J
A = D // P
G = 4
HEADS, DH = 16, 16
NT = B * T // P
BT = P // T
HC = P // DH
VW = BT * DH + BT
EPS = 1e-6


def build(nc, x, cond, w_ih, w_hh, b_ih, b_hh, w_emb, b_emb, g_norm, w_qkv, g_q, g_k, w_out, out, x1_dram):
    with ExitStack() as ctx:
        def sb(name, shape, dt=F32):
            return ctx.enter_context(nc.sbuf_tensor(name, shape, dt))

        def sem(name):
            return ctx.enter_context(nc.semaphore(name))

        X = sb("X", [P, T, C])
        Wih = sb("Wih", [P, A, 3 * D])
        Whh = sb("Whh", [P, A, 3 * D])
        Wemb = sb("Wemb", [P, A, 2 * D])
        Wqkv = sb("Wqkv", [P, A, 3 * D])
        Wout = sb("Wout", [P, A, D])
        bih = sb("bih", [1, 3 * D])
        bhh = sb("bhh", [1, 3 * D])
        bemb_jb = sb("bemb_jb", [P, 2, C])
        gnorm_jb = sb("gnorm_jb", [P, C])
        gq_p = sb("gq_p", [P, 1])
        gk_p = sb("gk_p", [P, 1])
        ident = sb("ident", [P, P])
        same_b = sb("same_b", [P, P])
        head_mask = sb("head_mask", [P, HC])
        ones3 = sb("ones3", [P, 32], BF16)
        bias3 = sb("bias3", [P, 4, D], BF16)
        bsum = sb("bsum", [1, 4, D])
        bhi = sb("bhi", [1, 4, D], BF16)
        blo = sb("blo", [1, 4, D])
        bmid = sb("bmid", [1, 4, D], BF16)
        eps_col = sb("eps_col", [P, 1])
        H = sb("H", [P, T + 1, C])
        hT = sb("hT", [P, 2, A, 32])
        xT = sb("xT", [P, 2, A, 32])
        r_sb = sb("r_sb", [P, C])
        z_sb = sb("z_sb", [P, C])
        n_sb = sb("n_sb", [P, C])
        rh = sb("rh", [P, C])
        npre = sb("npre", [P, C])
        zc = sb("zc", [P, C])
        zh = sb("zh", [P, C])
        u_sb = sb("u_sb", [P, C])
        X1 = sb("X1", [P, T, C])
        sq_junk = sb("sq_junk", [P, 2, C])
        ssq = sb("ssq", [P, T])
        ms = sb("ms", [P, T])
        half = sb("half", [P, T])
        rms = sb("rms", [P, T])
        gain = sb("gain", [P, C])
        shift = sb("shift", [P, C])
        y0 = sb("y0", [P, C])
        y = sb("y", [P, C])
        yT = sb("yT", [P, A, B, T])
        x1tok = sb("x1tok", [P, NT, D])
        sq = sb("sq", [P, 2 * D])
        qkss = sb("qkss", [P, 2 * HEADS])
        qkln = sb("qkln", [P, 2 * HEADS])
        qkr = sb("qkr", [P, 2 * HEADS])
        qkn = sb("qkn", [P, 2, 2 * D])
        qT = sb("qT", [P, 2, A, P])
        kT = sb("kT", [P, A, P])
        kblk = sb("kblk", [P, 2, A, HC, P])
        vblk = sb("vblk", [P, 3, HEADS, VW])
        mx = sb("mx", [P, HEADS])
        sm = sb("sm", [P, HEADS, T])
        ex = sb("ex", [P, HEADS * T])
        pT = sb("pT", [P, 2, HEADS * T])
        rden = sb("rden", [P, 4, BT])
        on = sb("on", [P, BT, 2, 2, DH])
        oT = sb("oT", [P, 2, A, BT, T])
        fin = sb("fin", [P, 2, D])

        banks = [ctx.enter_context(nc.psum_tensor(f"bank{i}", [P, 512], F32)) for i in range(8)]
        psA = [banks[0][:, 0:3 * C], banks[1][:, 0:3 * C]]
        psZ = [banks[2][:, 0:C], banks[3][:, 0:C]]
        psE = banks[7][:, 0:2 * C]
        psR = banks[6][:, 0:T]
        psQK = [banks[4], banks[5]]
        psV = banks[6]
        psT = banks[7]
        psS = [banks[0], banks[1]]
        psO = banks[2]
        psY = banks[3]

        d_cond, d_whh, d_wih, d_bias = sem("d_cond"), sem("d_whh"), sem("d_wih"), sem("d_bias")
        d_x = [sem(f"d_x{i}") for i in range(3)]
        d_emb, d_qkv, d_out_w, d_gqk = sem("d_emb"), sem("d_qkv"), sem("d_out_w"), sem("d_gqk")
        d_x1st, d_x1ld = sem("d_x1st"), sem("d_x1ld")
        d_res = [sem("d_res0"), sem("d_res1")]
        c_same, c_ident, c_mask, c_ones3, c_bias = (sem(s) for s in ("c_same", "c_ident", "c_mask", "c_ones3", "c_bias"))
        c_gk, c_wout, c_v = sem("c_gk"), sem("c_wout"), sem("c_v")
        p_A, p_Z = sem("p_A"), sem("p_Z")
        a_r, a_z, a_n = sem("a_r"), sem("a_z"), sem("a_n")
        v_rh, v_npre, v_zc, v_zh, v_u, v_h, v_hT, v_xT = (sem(s) for s in (
            "v_rh", "v_npre", "v_zc", "v_zh", "v_u", "v_h", "v_hT", "v_xT"))
        v_x1, a_ss, p_ss, v_ms, g_half, g_rms, v_y0, v_y, v_yT = (sem(s) for s in (
            "v_x1", "a_ss", "p_ss", "v_ms", "g_half", "g_rms", "v_y0", "v_y", "v_yT"))
        p_E, v_gs = sem("p_E"), sem("v_gs")
        p_qk, p_v, p_t, p_s, p_o, p_y = (sem(s) for s in ("p_qk", "p_v", "p_t", "p_s", "p_o", "p_y"))
        a_sq, a_ln, a_rr, a_q, a_k, a_kb, a_v, a_e = (sem(s) for s in (
            "a_sq", "a_ln", "a_rr", "a_q", "a_k", "a_kb", "a_v", "a_e"))
        v_ss, v_qkn, v_kb, v_mx, v_sm, v_pT, v_rd, v_on, v_oT, v_fin = (sem(s) for s in (
            "v_ss", "v_qkn", "v_kb", "v_mx", "v_sm", "v_pT", "v_rd", "v_on", "v_oT", "v_fin"))

        x_jb = x.rearrange("b t (j c) -> j b t c", j=J)
        x1_jb = x1_dram.rearrange("b t (j c) -> j b t c", j=J)
        cond_jb = cond.rearrange("b (j c) -> j b c", j=J)
        x1_tok = x1_dram.rearrange("(n b) t d -> (b t) n d", n=NT)
        out_tok = out.rearrange("(n b) t d -> n (b t) d", n=NT)

        def rows_T(w):
            return w.rearrange("(j a i) n -> a j i n", a=A, i=32)

        XCUT = [0, 4, 12, T]
        block = ctx.enter_context(nc.Block())

        @block.sync
        def _(sp):
            for j in range(J):
                sp.dma_start(H[32 * j:32 * j + 32, 0, :], cond_jb[j]).then_inc(d_cond, 16)
            for a in range(A):
                sp.dma_start(Whh[:, a, :], rows_T(w_hh)[a]).then_inc(d_whh, 16)
            for a in range(A):
                sp.dma_start(Wemb[:, a, :], rows_T(w_emb)[a]).then_inc(d_emb, 16)
            for j in range(J):
                jb = slice(32 * j, 32 * j + 32)
                sp.dma_start(gnorm_jb[jb, :], g_norm.rearrange("(j o c) -> j o c", j=J, o=1)[j].broadcast_to([32, C])).then_inc(d_emb, 16)
                sp.dma_start(bemb_jb[jb, :, :],
                             b_emb.rearrange("(s j o c) -> j o s c", j=J, s=2, o=1)[j].broadcast_to([32, 2, C])).then_inc(d_emb, 16)
            for a in range(A):
                sp.dma_start(Wqkv[:, a, :], rows_T(w_qkv)[a]).then_inc(d_qkv, 16)
                sp.dma_start(Wout[:, a, :], w_out[P * a:P * a + P, :]).then_inc(d_out_w, 16)
            for h in range(HC):
                sp.dma_start(gq_p[DH * h:DH * h + DH, :], g_q.rearrange("(d o) -> d o", o=1)).then_inc(d_gqk, 16)
                sp.dma_start(gk_p[DH * h:DH * h + DH, :], g_k.rearrange("(d o) -> d o", o=1)).then_inc(d_gqk, 16)
            for q in range(T // 8):
                sp.wait_ge(v_x1, 8 * q + 8)
                for j in range(J):
                    sp.dma_start(x1_jb[j][:, 8 * q:8 * q + 8, :], X1[32 * j:32 * j + 32, 8 * q:8 * q + 8, :]).then_inc(d_x1st, 16)
            sp.wait_ge(d_x1st, 16 * J * (T // 8))
            sp.dma_start(x1tok[:, :, :], x1_tok).then_inc(d_x1ld, 16)
            for n in range(NT):
                sp.wait_ge(v_fin, n + 1)
                sp.dma_start(out_tok[n], fin[:, n % 2, :]).then_inc(d_res[n % 2], 16)
            for k in range(2):
                sp.wait_ge(d_res[k], 16 * (NT // 2))

        @block.gpsimd
        def _(pool):
            pool.memset(ones3[:, :], 0.0).then_inc(c_ones3, 1)
            pool.wait_ge(c_ones3, 1)
            for r in range(3):
                pool.memset(ones3[32 * r:32 * r + 1, :], 1.0).then_inc(c_ones3, 1)
                pool.wait_ge(c_ones3, 2 + r)
            pool.memset(half[:, :], -0.5).then_inc(g_half, 1)
            pool.memset(eps_col[:, :], EPS).then_inc(g_half, 1)
            pool.wait_ge(g_half, 2)
            pool.memset(same_b[:, :], 0.0).then_inc(c_same, 1)
            for k in range(J):
                pool.wait_ge(c_same, 1 + k)
                v = same_b[:, :].rearrange("p (j b) -> p j b", j=J)
                pool.affine_select(out=v, in_=v, compare_op=ALU.not_equal, fill=1.0, base=-32 * k,
                                   pattern=[[0, J], [-1, 32]], channel_multiplier=1).then_inc(c_same, 1)
            pool.wait_ge(c_same, 1 + J)
            pool.memset(ident[:, :], 0.0).then_inc(c_ident, 1)
            pool.wait_ge(c_ident, 1)
            pool.affine_select(out=ident[:, :], in_=ident[:, :], compare_op=ALU.not_equal, fill=1.0, base=0,
                               pattern=[[-1, P]], channel_multiplier=1).then_inc(c_ident, 1)
            pool.wait_ge(c_ident, 2)
            pool.memset(head_mask[:, :], 1.0).then_inc(c_mask, 1)
            pool.wait_ge(c_mask, 1)
            pool.affine_select(out=head_mask[:, :], in_=head_mask[:, :], compare_op=ALU.is_ge, fill=0.0, base=0,
                               pattern=[[-DH, HC]], channel_multiplier=1).then_inc(c_mask, 1)
            pool.wait_ge(c_mask, 2)
            pool.affine_select(out=head_mask[:, :], in_=head_mask[:, :], compare_op=ALU.is_ge, fill=0.0, base=DH - 1,
                               pattern=[[DH, HC]], channel_multiplier=-1).then_inc(c_mask, 1)
            pool.wait_ge(c_mask, 3)
            for k in range(3):
                pool.memset(vblk[:, k, :, :], 0.0).then_inc(c_v, 1)
                pool.wait_ge(c_v, k + 1)
            for b in range(BT):
                for k in range(3):
                    pool.memset(vblk[32 * b:32 * b + 32, k, :, BT * DH + b:BT * DH + b + 1], 1.0).then_inc(c_v, 1)
            pool.wait_ge(c_v, 3 + 3 * BT)
            for q in range(T // G):
                pool.wait_ge(v_ms, q + 1)
                pool.tensor_tensor(rms[:, G * q:G * q + G], ms[:, G * q:G * q + G], half[:, G * q:G * q + G],
                                   ALU.pow).then_inc(g_rms, 1)

        @block.scalar
        def _(act):
            act.dma_start(bih[:, :], b_ih.rearrange("(o n) -> o n", o=1)).then_inc(d_bias, 16)
            act.dma_start(bhh[:, :], b_hh.rearrange("(o n) -> o n", o=1)).then_inc(d_bias, 16)
            for part in range(3):
                for j in range(J):
                    s = slice(XCUT[part], XCUT[part + 1])
                    act.dma_start(X[32 * j:32 * j + 32, s, :], x_jb[j][:, s, :]).then_inc(d_x[part], 16)
                if part == 0:
                    for a in range(A):
                        act.dma_start(Wih[:, a, :], rows_T(w_ih)[a]).then_inc(d_wih, 16)

            def sum_squares(t):
                act.wait_ge(v_x1, t + 1)
                if t >= 2:
                    act.wait_ge(a_ss, t - 1)
                act.activation(sq_junk[:, t % 2, :], X1[:, t, :], ACT.Square, accum_out=ssq[:, t:t + 1]).then_inc(a_ss, 1)

            for t in range(T):
                act.wait_ge(p_A, t + 1)
                if t >= 1:
                    act.wait_ge(v_rh, t)
                act.activation(r_sb[:, :], psA[t % 2][:, 0:C], ACT.Sigmoid).then_inc(a_r, 1)
                act.wait_ge(p_Z, t + 1)
                if t >= 1:
                    act.wait_ge(v_zh, t)
                act.activation(z_sb[:, :], psZ[t % 2], ACT.Sigmoid).then_inc(a_z, 1)
                act.wait_ge(v_npre, t + 1)
                if t >= 1:
                    act.wait_ge(v_u, t)
                act.activation(n_sb[:, :], npre[:, :], ACT.Tanh).then_inc(a_n, 1)
                if t >= 1:
                    sum_squares(t - 1)
            sum_squares(T - 1)

            def squares(n):
                act.wait_ge(p_qk, n + 1)
                if n >= 1:
                    act.wait_ge(v_ss, n)
                act.activation(sq[:, :], psQK[n % 2][:, :], ACT.Square).then_inc(a_sq, 1)

            def rsqrt(n):
                act.wait_ge(g_half, 2)
                act.wait_ge(v_ss, n + 1)
                act.activation(qkln[:, :], qkss[:, :], ACT.Ln, scale=1.0 / DH, bias=eps_col[:, :]).then_inc(a_ln, 1)
                act.wait_ge(a_ln, n + 1)
                if n >= 1:
                    act.wait_ge(v_qkn, n)
                act.activation(qkr[:, :], qkln[:, :], ACT.Exp, scale=-0.5).then_inc(a_rr, 1)

            def v_operand(n):
                act.wait_ge(p_v, n + 1)
                act.wait_ge(c_v, 3 + 3 * BT)
                if n >= 3:
                    act.wait_ge(p_o, n - 2)
                for b in range(BT):
                    rows = slice(32 * b, 32 * b + 32)
                    act.activation(vblk[rows, n % 3, :, DH * b:DH * b + DH],
                                   psV[rows, 0:D].rearrange("p (h d) -> p h d", d=DH), ACT.Copy).then_inc(a_v, 1)

            def qk_T(n):
                act.wait_ge(p_t, n + 1)
                act.wait_ge(c_gk, 2)
                if n >= 2:
                    act.wait_ge(p_s, n - 1)
                if n >= 1:
                    act.wait_ge(v_kb, n)
                act.activation(kT[:, :, :], psT[:, 2 * P:4 * P].rearrange("p (a t) -> p a t", a=A), ACT.Copy).then_inc(a_k, 1)
                act.activation(qT[:, n % 2, :, :], psT[:, 0:2 * P].rearrange("p (a t) -> p a t", a=A), ACT.Copy,
                               scale=gq_p[:, 0:1]).then_inc(a_q, 1)
                act.wait_ge(a_k, n + 1)
                for h in range(HC // 2):
                    act.activation(kblk[:, n % 2, :, h, :], kT[:, :, :], ACT.Copy,
                                   scale=head_mask[:, h:h + 1]).then_inc(a_kb, 1)

            def exps(n):
                act.wait_ge(v_sm, n + 1)
                if n >= 1:
                    act.wait_ge(v_pT, n)
                act.activation(ex[:, :], sm[:, :, :].rearrange("p h k -> p (h k)"), ACT.Exp).then_inc(a_e, 1)

            for n in range(NT + 2):
                if n < NT:
                    squares(n)
                if n >= 2:
                    exps(n - 2)
                if n < NT:
                    rsqrt(n)
                    v_operand(n)
                if 1 <= n <= NT:
                    qk_T(n - 1)

        @block.vector
        def _(dve):
            dve.wait_ge(d_bias, 32)
            dve.tensor_tensor(bsum[:, 0, :], bih[:, 0:D], bhh[:, 0:D], ALU.add).then_inc(c_bias, 1)
            dve.tensor_tensor(bsum[:, 3, :], bih[:, D:2 * D], bhh[:, D:2 * D], ALU.add).then_inc(c_bias, 1)
            dve.tensor_copy(bsum[:, 1, :], bhh[:, 2 * D:3 * D]).then_inc(c_bias, 1)
            dve.tensor_copy(bsum[:, 2, :], bih[:, 2 * D:3 * D]).then_inc(c_bias, 1)
            dve.wait_ge(c_bias, 4)
            dve.tensor_copy(bhi[:, :, :], bsum[:, :, :]).then_inc(c_bias, 1)
            dve.wait_ge(c_bias, 5)
            dve.tensor_tensor(blo[:, :, :], bsum[:, :, :], bhi[:, :, :], ALU.subtract).then_inc(c_bias, 1)
            dve.wait_ge(c_bias, 6)
            dve.tensor_copy(bmid[:, :, :], blo[:, :, :]).then_inc(c_bias, 1)
            dve.memset(bias3[:, :, :], 0.0).then_inc(c_bias, 1)
            dve.wait_ge(c_bias, 8)
            dve.tensor_copy(bias3[0:1, :, :], bhi[:, :, :]).then_inc(c_bias, 1)
            dve.tensor_copy(bias3[32:33, :, :], bmid[:, :, :]).then_inc(c_bias, 1)
            dve.tensor_tensor(bias3[64:65, :, :], blo[:, :, :], bmid[:, :, :], ALU.subtract).then_inc(c_bias, 1)

            def part_of(t):
                return 0 if t < XCUT[1] else 1 if t < XCUT[2] else 2

            def x_transpose(t):
                dve.wait_ge(d_x[part_of(t)], 16 * J)
                if t >= 2:
                    dve.wait_ge(p_Z, t - 1)
                dve.transpose(xT[:, t % 2, :, :].rearrange("p a b -> p (a b)"), X[:, t, :]).then_inc(v_xT, 1)

            dve.wait_ge(d_cond, 16 * J)
            dve.transpose(hT[:, 0, :, :].rearrange("p a b -> p (a b)"), H[:, 0, :]).then_inc(v_hT, 1)
            x_transpose(0)
            x_transpose(1)
            dve.wait_ge(d_emb, 16 * (A + 2 * J))
            dve.wait_ge(p_E, 1)
            dve.scalar_tensor_tensor(out=gain[:, :], in0=psE[:, 0:C], scalar=1.0, in1=bemb_jb[:, 0, :],
                                     op0=ALU.add, op1=ALU.add).then_inc(v_gs, 1)
            dve.tensor_tensor(shift[:, :], psE[:, C:2 * C], bemb_jb[:, 1, :], ALU.add).then_inc(v_gs, 1)
            dve.wait_ge(v_gs, 1)
            dve.tensor_tensor(gain[:, :], gain[:, :], gnorm_jb[:, :], ALU.mult).then_inc(v_gs, 1)

            def residual(t):
                dve.wait_ge(v_h, t + 1)
                dve.tensor_tensor(X1[:, t, :], X[:, t, :], H[:, t + 1, :], ALU.add).then_inc(v_x1, 1)

            def mean_square(q):
                dve.wait_ge(p_ss, q + 1)
                dve.tensor_scalar(ms[:, G * q:G * q + G], psR[:, G * q:G * q + G], 1.0 / D, EPS,
                                  ALU.mult, ALU.add).then_inc(v_ms, 1)

            def norm(t):
                dve.wait_ge(g_rms, t // G + 1)
                dve.wait_ge(v_x1, t + 1)
                dve.wait_ge(v_gs, 3)
                dve.scalar_tensor_tensor(out=y0[:, :], in0=X1[:, t, :], scalar=rms[:, t:t + 1], in1=gain[:, :],
                                         op0=ALU.mult, op1=ALU.mult).then_inc(v_y0, 1)
                dve.wait_ge(v_y0, t + 1)
                dve.tensor_tensor(y[:, :], y0[:, :], shift[:, :], ALU.add).then_inc(v_y, 1)
                dve.wait_ge(v_y, t + 1)
                dve.transpose(yT[:, :, :, t], y[:, :]).then_inc(v_yT, 1)

            LAG = G + 2
            for t in range(T):
                h_new = H[:, t + 1, :]
                dve.wait_ge(a_r, t + 1)
                dve.tensor_tensor(rh[:, :], psA[t % 2][:, C:2 * C], r_sb[:, :], ALU.mult).then_inc(v_rh, 1)
                dve.wait_ge(v_rh, t + 1)
                dve.tensor_tensor(npre[:, :], psA[t % 2][:, 2 * C:3 * C], rh[:, :], ALU.add).then_inc(v_npre, 1)
                dve.wait_ge(a_z, t + 1)
                dve.tensor_scalar(zc[:, :], z_sb[:, :], -1.0, 1.0, ALU.mult, ALU.add).then_inc(v_zc, 1)
                dve.tensor_tensor(zh[:, :], z_sb[:, :], H[:, t, :], ALU.mult).then_inc(v_zh, 1)
                dve.wait_ge(v_zc, t + 1)
                dve.wait_ge(a_n, t + 1)
                dve.tensor_tensor(u_sb[:, :], zc[:, :], n_sb[:, :], ALU.mult).then_inc(v_u, 1)
                dve.wait_ge(v_u, t + 1)
                dve.tensor_tensor(h_new, u_sb[:, :], zh[:, :], ALU.add).then_inc(v_h, 1)
                dve.wait_ge(v_h, t + 1)
                if t < T - 1:
                    dve.transpose(hT[:, (t + 1) % 2, :, :].rearrange("p a b -> p (a b)"), h_new).then_inc(v_hT, 1)
                residual(t)
                if t + 2 < T:
                    x_transpose(t + 2)
                if t % G == 1 and t > G:
                    mean_square(t // G - 1)
                if t >= LAG + 1:
                    norm(t - LAG - 1)
            mean_square(T // G - 1)
            for t in range(T - LAG - 1, T):
                norm(t)

            dve.wait_ge(d_gqk, 16 * 2 * HC)
            dve.wait_ge(c_mask, 3)
            dve.wait_ge(c_ident, 2)
            dve.tensor_scalar(gq_p[:, :], gq_p[:, :], DH ** -0.5, None, ALU.mult).then_inc(c_gk, 1)
            dve.tensor_scalar(head_mask[:, :], head_mask[:, :], gk_p[:, 0:1], None, ALU.mult).then_inc(c_gk, 1)
            dve.wait_ge(d_out_w, 16 * A)
            for a in range(A):
                dve.tensor_tensor(Wout[:, a, P * a:P * a + P], Wout[:, a, P * a:P * a + P], ident[:, :],
                                  ALU.add).then_inc(c_wout, 1)

            def qk_norm(n):
                dve.wait_ge(a_sq, n + 1)
                if n >= 1:
                    dve.wait_ge(a_ln, n)
                dve.tensor_reduce(qkss[:, :], sq[:, :].rearrange("p (h d) -> p h d", d=DH), AX.X, ALU.add).then_inc(v_ss, 1)

            def qk_scale(n):
                dve.wait_ge(a_rr, n + 1)
                if n >= 2:
                    dve.wait_ge(p_t, n - 1)
                dve.tensor_tensor(qkn[:, n % 2, :].rearrange("p (h d) -> p h d", d=DH),
                                  psQK[n % 2][:, :].rearrange("p (h d) -> p h d", d=DH),
                                  qkr[:, :].unsqueeze(2).broadcast_to([P, 2 * HEADS, DH]), ALU.mult).then_inc(v_qkn, 1)

            def k_blocks(n):
                dve.wait_ge(a_k, n + 1)
                dve.wait_ge(c_gk, 2)
                if n >= 2:
                    dve.wait_ge(p_s, n - 1)
                for h in range(HC // 2, HC):
                    last = dve.tensor_scalar(kblk[:, n % 2, :, h, :], kT[:, :, :], head_mask[:, h:h + 1], None, ALU.mult)
                last.then_inc(v_kb, 1)

            def softmax_shift(n):
                S = psS[n % 2][:, :].rearrange("p (h k) -> p h k", k=T)
                dve.wait_ge(p_s, n + 1)
                dve.tensor_reduce(mx[:, :], S, AX.X, ALU.max).then_inc(v_mx, 1)
                dve.wait_ge(v_mx, n + 1)
                if n >= 1:
                    dve.wait_ge(a_e, n)
                dve.tensor_tensor(sm[:, :, :], S, mx[:, :].unsqueeze(2).broadcast_to([P, HEADS, T]),
                                  ALU.subtract).then_inc(v_sm, 1)

            def p_transpose(n):
                dve.wait_ge(a_e, n + 1)
                if n >= 2:
                    dve.wait_ge(p_o, n - 1)
                dve.transpose(pT[:, n % 2, :], ex[:, :]).then_inc(v_pT, 1)

            def o_norm(n):
                O = psO[:, 0:4 * VW].rearrange("p (c w) -> p c w", w=VW)
                dve.wait_ge(p_o, n + 1)
                dve.reciprocal(rden[:, :, :], O[:, :, BT * DH:VW]).then_inc(v_rd, 1)
                dve.wait_ge(v_rd, n + 1)
                for s in range(4):
                    last = dve.tensor_tensor(on[:, :, s // 2, s % 2, :],
                                             O[:, s, 0:BT * DH].rearrange("p (b d) -> p b d", d=DH),
                                             rden[:, s, :].unsqueeze(2).broadcast_to([P, BT, DH]), ALU.mult)
                last.then_inc(v_on, 1)
                dve.wait_ge(v_on, n + 1)
                if n >= 2:
                    dve.wait_ge(p_y, n - 1)
                for a in range(A):
                    last = dve.transpose(oT[:, n % 2, a, :, :],
                                         on[:, :, a, :, :].rearrange("p b s d -> p b (s d)"))
                last.then_inc(v_oT, 1)

            def last_residual(n):
                dve.wait_ge(p_y, n + 1)
                dve.wait_ge(d_x1ld, 16)
                if n >= 2:
                    dve.wait_ge(d_res[n % 2], 16 * (n // 2))
                dve.tensor_tensor(fin[:, n % 2, :], psY[:, 0:D], x1tok[:, n, :], ALU.add).then_inc(v_fin, 1)

            for n in range(NT + 4):
                if n < NT:
                    qk_norm(n)
                if 2 <= n < NT + 2:
                    softmax_shift(n - 2)
                if n < NT:
                    qk_scale(n)
                if 1 <= n <= NT:
                    k_blocks(n - 1)
                if 2 <= n < NT + 2:
                    p_transpose(n - 2)
                if 3 <= n < NT + 3:
                    o_norm(n - 3)
                if n >= 4:
                    last_residual(n - 4)

        @block.tensor
        def _(pe):
            def gate(out_ps, cols, stationary, w, sl, start, stop):
                for j in range(J):
                    rows = slice(32 * j, 32 * j + 32)
                    last = pe.matmul(out_ps[rows, cols], stationary, w[:, sl[0], sl[1], C * j:C * j + C],
                                     start=start, stop=stop, skip_group_check=True)
                return last

            wih = Wih[:, :, :].rearrange("p a (g n) -> p a g n", g=3)
            whh = Whh[:, :, :].rearrange("p a (g n) -> p a g n", g=3)
            wemb = Wemb[:, :, :].rearrange("p a (g n) -> p a g n", g=2)

            def x_gates(t):
                pa, pz = psA[t % 2], psZ[t % 2]
                for j in range(J):
                    rows = slice(32 * j, 32 * j + 32)
                    pe.matmul(pa[rows, :].rearrange("p (g c) -> p g c", g=3), ones3[:, :], bias3[:, 0:3, C * j:C * j + C],
                              start=True, stop=False, skip_group_check=True)
                for j in range(J):
                    rows = slice(32 * j, 32 * j + 32)
                    pe.matmul(pz[rows, :], ones3[:, :], bias3[:, 3, C * j:C * j + C],
                              start=True, stop=False, skip_group_check=True)
                pe.wait_ge(v_xT, t + 1)
                for a in range(A):
                    for j in range(J):
                        rows = slice(32 * j, 32 * j + 32)
                        pe.matmul(pa[rows, :].rearrange("p (g c) -> p g c", g=3)[:, 0::2, :], xT[:, t % 2, a, :],
                                  wih[:, a, 0::2, C * j:C * j + C], start=False, stop=False, skip_group_check=True)
                for a in range(A):
                    for j in range(J):
                        rows = slice(32 * j, 32 * j + 32)
                        pe.matmul(pz[rows, :], xT[:, t % 2, a, :], wih[:, a, 1, C * j:C * j + C],
                                  start=False, stop=False, skip_group_check=True)

            def h_gates(t):
                pa, pz = psA[t % 2], psZ[t % 2]
                pe.wait_ge(v_hT, t + 1)
                for a in range(A):
                    for j in range(J):
                        rows = slice(32 * j, 32 * j + 32)
                        last = pe.matmul(pa[rows, 0:2 * C].rearrange("p (g c) -> p g c", g=2), hT[:, t % 2, a, :],
                                         whh[:, a, 0::2, C * j:C * j + C], start=False, stop=(a == A - 1),
                                         skip_group_check=True)
                last.then_inc(p_A, 1)
                for a in range(A):
                    for j in range(J):
                        rows = slice(32 * j, 32 * j + 32)
                        last = pe.matmul(pz[rows, :], hT[:, t % 2, a, :], whh[:, a, 1, C * j:C * j + C],
                                         start=False, stop=(a == A - 1), skip_group_check=True)
                last.then_inc(p_Z, 1)

            pe.wait_ge(c_ones3, 4)
            pe.wait_ge(c_bias, 11)
            pe.wait_ge(d_wih, 16 * A)
            x_gates(0)
            pe.wait_ge(d_whh, 16 * A)
            for t in range(T):
                h_gates(t)
                if t == 0:
                    pe.wait_ge(d_emb, 16 * (A + 2 * J))
                    for a in range(A):
                        for j in range(J):
                            rows = slice(32 * j, 32 * j + 32)
                            last = pe.matmul(psE[rows, :].rearrange("p (g c) -> p g c", g=2), hT[:, 0, a, :],
                                             wemb[:, a, :, C * j:C * j + C], start=(a == 0), stop=(a == A - 1),
                                             skip_group_check=True)
                    last.then_inc(p_E, 1)
                if t + 1 < T:
                    if t >= 1:
                        pe.wait_ge(a_z, t)
                        pe.wait_ge(v_npre, t)
                    x_gates(t + 1)
                if t % G == 0 and t > 0:
                    q = t // G - 1
                    if q == 0:
                        pe.wait_ge(c_same, 1 + J)
                    pe.wait_ge(a_ss, G * q + G)
                    if q >= 1:
                        pe.wait_ge(v_ms, q)
                    pe.matmul(psR[:, G * q:G * q + G], same_b[:, :], ssq[:, G * q:G * q + G],
                              start=True, stop=True, skip_group_check=True).then_inc(p_ss, 1)
            q = T // G - 1
            pe.wait_ge(a_ss, T)
            pe.wait_ge(v_ms, q)
            pe.matmul(psR[:, G * q:G * q + G], same_b[:, :], ssq[:, G * q:G * q + G],
                      start=True, stop=True, skip_group_check=True).then_inc(p_ss, 1)

            def project(n):
                if n == 0:
                    pe.wait_ge(d_qkv, 16 * A)
                    pe.wait_ge(v_yT, T)
                if n >= 2:
                    pe.wait_ge(v_qkn, n - 1)
                for a in range(A):
                    toks = yT[:, a, BT * n:BT * n + BT, :].rearrange("p b t -> p (b t)")
                    last = pe.matmul(psQK[n % 2][:, :], toks, Wqkv[:, a, 0:2 * D], start=(a == 0), stop=(a == A - 1))
                last.then_inc(p_qk, 1)
                if n >= 1:
                    pe.wait_ge(a_v, BT * n)
                for a in range(A):
                    toks = yT[:, a, BT * n:BT * n + BT, :].rearrange("p b t -> p (b t)")
                    last = pe.matmul(psV[:, 0:D], toks, Wqkv[:, a, 2 * D:3 * D], start=(a == 0), stop=(a == A - 1))
                last.then_inc(p_v, 1)

            def transposes(n):
                pe.wait_ge(v_qkn, n + 1)
                if n >= 1:
                    pe.wait_ge(a_q, n)
                for c in range(4):
                    last = pe.transpose(psT[:, P * c:P * c + P], qkn[:, n % 2, P * c:P * c + P], ident[:, :])
                last.then_inc(p_t, 1)

            def scores(n):
                pe.wait_ge(a_q, n + 1)
                pe.wait_ge(a_kb, (HC // 2) * (n + 1))
                pe.wait_ge(v_kb, n + 1)
                if n >= 2:
                    pe.wait_ge(v_sm, n - 1)
                for a in range(A):
                    for b in range(BT):
                        cols = slice(32 * b, 32 * b + 32)
                        last = pe.matmul(psS[n % 2][cols, D * a:D * a + D].rearrange("p (h k) -> p h k", k=T),
                                         qT[:, n % 2, a, cols], kblk[:, n % 2, a, :, cols], start=True, stop=True)
                last.then_inc(p_s, 1)

            def attend(n):
                pe.wait_ge(v_pT, n + 1)
                pe.wait_ge(a_v, BT * (n + 1))
                if n >= 1:
                    pe.wait_ge(v_on, n)
                for cs in range(4):
                    for g in range(4):
                        h = 8 * (cs // 2) + 2 * g + cs % 2
                        last = pe.matmul(psO[32 * g:32 * g + 32, VW * cs:VW * cs + VW], pT[:, n % 2, T * h:T * h + T],
                                         vblk[:, n % 3, h, :], start=True, stop=True)
                last.then_inc(p_o, 1)

            def out_project(n):
                pe.wait_ge(v_oT, n + 1)
                pe.wait_ge(c_wout, A)
                if n >= 1:
                    pe.wait_ge(v_fin, n)
                for a in range(A):
                    last = pe.matmul(psY[:, 0:D], oT[:, n % 2, a, :, :].rearrange("p b t -> p (b t)"), Wout[:, a, :],
                                     start=(a == 0), stop=(a == A - 1))
                last.then_inc(p_y, 1)

            pe.wait_ge(c_ident, 2)
            for n in range(NT + 4):
                if n < NT:
                    project(n)
                if 2 <= n < NT + 2:
                    scores(n - 2)
                if 3 <= n < NT + 3:
                    attend(n - 3)
                if n >= 4:
                    out_project(n - 4)
                if n < NT:
                    transposes(n)


_INS = ["x", "cond_2048", "L0_cond_W_ih", "L0_cond_W_hh", "L0_cond_b_ih", "L0_cond_b_hh", "L1_cond_W_emb",
        "L1_cond_b_emb", "L1_cond_g_norm", "L1_cond_W_qkv", "L1_cond_g_q", "L1_cond_g_k", "L1_cond_W_out"]


def kernel(**inputs):
    import numpy as _np
    import concourse.bacc as _bacc
    from concourse import mybir as _mybir
    from concourse.bass_utils import run_bass_kernel_spmd as _run

    nc = _bacc.Bacc("TRN2", target_bir_lowering=False, num_devices=1)
    arrays, args = {}, []
    for name in _INS:
        a = _np.ascontiguousarray(inputs[name])
        arrays[f"in_{name}_dram"] = a
        args.append(nc.dram_tensor(f"in_{name}_dram", a.shape, _mybir.dt.from_np(a.dtype), kind="ExternalInput").ap())
    args.append(nc.dram_tensor("out_0_dram", (B, T, D), F32, kind="ExternalOutput").ap())
    args.append(nc.dram_tensor("x1_scratch", (B, T, D), F32, kind="Internal").ap())
    build(nc, *args)
    r = _run(nc, [arrays], core_ids=[0])
    return r.results[0]["out_0_dram"]
```

```python
from contextlib import ExitStack

import concourse.bass as bass
from concourse import mybir

F32 = mybir.dt.float32
BF16 = mybir.dt.bfloat16
ALU = mybir.AluOpType
ACT = mybir.ActivationFunctionType
AX = mybir.AxisListType

P = 128
B, T, D = 32, 32, 256
J = 4
C = D // J
A = D // P
G = 4
HEADS, DH = 16, 16
NT = B * T // P
BT = P // T
HC = P // DH
NB = 4
LAG_T, LAG_S, LAG_PV, LAG_Y = NB, NB + 1, NT, NT + 1
VW = BT * DH + BT
EPS = 1e-6
EMB_STEP = 3
WARM = 12


def batch(k):
    return slice(NB * k, NB * k + NB)


def build(nc, x, cond, w_ih, w_hh, b_ih, b_hh, w_emb, b_emb, g_norm, w_qkv, g_q, g_k, w_out, out, x1_dram):
    with ExitStack() as ctx:
        def sb(name, shape, dt=F32):
            return ctx.enter_context(nc.sbuf_tensor(name, shape, dt))

        def sem(name):
            return ctx.enter_context(nc.semaphore(name))

        X = sb("X", [P, T, C])
        Wih = sb("Wih", [P, A, 3 * D])
        Whh = sb("Whh", [P, A, 3 * D])
        Wemb = sb("Wemb", [P, A, 2 * D])
        Wqkv = sb("Wqkv", [P, A, 3 * D])
        Wout = sb("Wout", [P, A, D])
        bih = sb("bih", [1, 3 * D])
        bhh = sb("bhh", [1, 3 * D])
        bemb_jb = sb("bemb_jb", [P, 2, C])
        gnorm_jb = sb("gnorm_jb", [P, C])
        gq_p = sb("gq_p", [P, 1])
        gk_p = sb("gk_p", [P, 1])
        ident = sb("ident", [P, P])
        same_b = sb("same_b", [P, P])
        head_mask = sb("head_mask", [P, HC])
        ones3 = sb("ones3", [P, 32], BF16)
        bias3 = sb("bias3", [P, 4, D], BF16)
        bsum = sb("bsum", [1, 4, D])
        bhi = sb("bhi", [1, 4, D], BF16)
        blo = sb("blo", [1, 4, D])
        bmid = sb("bmid", [1, 4, D], BF16)
        warm = sb("warm", [P, 512])
        H = sb("H", [P, T + 1, C])
        hT = sb("hT", [P, 2, A, 32])
        condT = sb("condT", [P, A, 32])
        xT = sb("xT", [P, 2, A, 32])
        r_sb = sb("r_sb", [P, C])
        z_sb = sb("z_sb", [P, C])
        n_sb = sb("n_sb", [P, C])
        rh = sb("rh", [P, C])
        zh = sb("zh", [P, C])
        u_sb = sb("u_sb", [P, C])
        X1 = sb("X1", [P, T, C])
        sq_junk = sb("sq_junk", [P, 2, C])
        ssq = sb("ssq", [P, T])
        ms = sb("ms", [P, T])
        half = sb("half", [P, T])
        rms = sb("rms", [P, T])
        gain = sb("gain", [P, C])
        shift = sb("shift", [P, C])
        y0 = sb("y0", [P, C])
        y = sb("y", [P, C])
        yT = sb("yT", [P, A, B, T])
        x1tok = sb("x1tok", [P, NT, D])
        sq = sb("sq", [P, 2 * D])
        qk = sb("qk", [P, NT, 2 * D])
        qkss = sb("qkss", [P, NT, 2 * HEADS])
        qkms = sb("qkms", [P, NT, 2 * HEADS])
        qkinv = sb("qkinv", [P, NT, 2 * HEADS])
        qkr = sb("qkr", [P, NT, 2 * HEADS])
        qkn = sb("qkn", [P, 2, 2 * D])
        qT = sb("qT", [P, 2, A, P])
        kT = sb("kT", [P, A, P])
        kblk = sb("kblk", [P, 2, A, HC, P])
        vblk = sb("vblk", [P, 3, HEADS, VW])
        mx = sb("mx", [P, HEADS])
        sm = sb("sm", [P, 3, HEADS, T])
        ex = sb("ex", [P, HEADS * T])
        pT = sb("pT", [P, 2, HEADS * T])
        rden = sb("rden", [P, 4, BT])
        on = sb("on", [P, BT, 2, 2, DH])
        oT = sb("oT", [P, 2, A, BT, T])
        fin = sb("fin", [P, 2, D])

        banks = [ctx.enter_context(nc.psum_tensor(f"bank{i}", [P, 512], F32)) for i in range(8)]
        psR = [banks[0][:, 0:2 * C], banks[1][:, 0:2 * C]]
        psN = banks[2][:, 0:C]
        psZ = banks[3][:, 0:C]
        npre = banks[4][:, 0:C]
        psE = banks[7][:, 0:2 * C]
        psM = banks[6][:, 0:T]
        psQK = [banks[4], banks[5]]
        psV = banks[6]
        psT = banks[7]
        psS = [banks[0], banks[1]]
        psO = banks[2]
        psY = banks[3]

        d_cond, d_whh, d_wih, d_bias = sem("d_cond"), sem("d_whh"), sem("d_wih"), sem("d_bias")
        d_x = [sem(f"d_x{i}") for i in range(3)]
        d_emb, d_qkv, d_out_w, d_gqk = sem("d_emb"), sem("d_qkv"), sem("d_out_w"), sem("d_gqk")
        d_x1st, d_x1ld = sem("d_x1st"), sem("d_x1ld")
        d_res = [sem("d_res0"), sem("d_res1")]
        c_warm, c_condT = sem("c_warm"), sem("c_condT")
        c_same, c_ident, c_mask, c_ones3, c_bias = (sem(s) for s in ("c_same", "c_ident", "c_mask", "c_ones3", "c_bias"))
        c_gk, c_wout, c_v = sem("c_gk"), sem("c_wout"), sem("c_v")
        p_r, p_hn, p_Z = sem("p_r"), sem("p_hn"), sem("p_Z")
        a_r, a_z, a_n = sem("a_r"), sem("a_z"), sem("a_n")
        v_rh, v_npre, v_zh, v_u, v_h, v_hT, v_xT = (sem(s) for s in (
            "v_rh", "v_npre", "v_zh", "v_u", "v_h", "v_hT", "v_xT"))
        v_x1, a_ss, p_ss, v_ms, g_half, g_rms, v_y0, v_y, v_yT = (sem(s) for s in (
            "v_x1", "a_ss", "p_ss", "v_ms", "g_half", "g_rms", "v_y0", "v_y", "v_yT"))
        p_E, v_gs = sem("p_E"), sem("v_gs")
        p_qk, p_v, p_t, p_s, p_o, p_y = (sem(s) for s in ("p_qk", "p_v", "p_t", "p_s", "p_o", "p_y"))
        a_sq, a_qk, a_rr, a_q, a_k, a_kb, a_v, a_e = (sem(s) for s in (
            "a_sq", "a_qk", "a_rr", "a_q", "a_k", "a_kb", "a_v", "a_e"))
        v_ms2, v_inv, v_ss, v_qkn, v_kb, v_mx, v_sm, v_pT, v_rd, v_on, v_oT, v_fin = (sem(s) for s in (
            "v_ms2", "v_inv", "v_ss", "v_qkn", "v_kb", "v_mx", "v_sm", "v_pT", "v_rd", "v_on", "v_oT", "v_fin"))

        x_jb = x.rearrange("b t (j c) -> j b t c", j=J)
        x1_jb = x1_dram.rearrange("b t (j c) -> j b t c", j=J)
        cond_jb = cond.rearrange("b (j c) -> j b c", j=J)
        x1_tok = x1_dram.rearrange("(n b) t d -> (b t) n d", n=NT)
        out_tok = out.rearrange("(n b) t d -> n (b t) d", n=NT)

        def rows_T(w):
            return w.rearrange("(j a i) n -> a j i n", a=A, i=32)

        XCUT = [0, 4, 12, T]
        block = ctx.enter_context(nc.Block())

        @block.sync
        def _(sp):
            for j in range(J):
                sp.dma_start(H[32 * j:32 * j + 32, 0, :], cond_jb[j]).then_inc(d_cond, 16)
            for a in range(A):
                sp.dma_start(Whh[:, a, :], rows_T(w_hh)[a]).then_inc(d_whh, 16)
            for a in range(A):
                sp.dma_start(Wemb[:, a, :], rows_T(w_emb)[a]).then_inc(d_emb, 16)
            for j in range(J):
                jb = slice(32 * j, 32 * j + 32)
                sp.dma_start(gnorm_jb[jb, :], g_norm.rearrange("(j o c) -> j o c", j=J, o=1)[j].broadcast_to([32, C])).then_inc(d_emb, 16)
                sp.dma_start(bemb_jb[jb, :, :],
                             b_emb.rearrange("(s j o c) -> j o s c", j=J, s=2, o=1)[j].broadcast_to([32, 2, C])).then_inc(d_emb, 16)
            for a in range(A):
                sp.dma_start(Wqkv[:, a, :], rows_T(w_qkv)[a]).then_inc(d_qkv, 16)
                sp.dma_start(Wout[:, a, :], w_out[P * a:P * a + P, :]).then_inc(d_out_w, 16)
            for h in range(HC):
                sp.dma_start(gq_p[DH * h:DH * h + DH, :], g_q.rearrange("(d o) -> d o", o=1)).then_inc(d_gqk, 16)
                sp.dma_start(gk_p[DH * h:DH * h + DH, :], g_k.rearrange("(d o) -> d o", o=1)).then_inc(d_gqk, 16)
            for q in range(T // 8):
                sp.wait_ge(v_x1, 8 * q + 8)
                for j in range(J):
                    sp.dma_start(x1_jb[j][:, 8 * q:8 * q + 8, :], X1[32 * j:32 * j + 32, 8 * q:8 * q + 8, :]).then_inc(d_x1st, 16)
            sp.wait_ge(d_x1st, 16 * J * (T // 8))
            sp.dma_start(x1tok[:, :, :], x1_tok).then_inc(d_x1ld, 16)
            for n in range(NT):
                sp.wait_ge(v_fin, n + 1)
                sp.dma_start(out_tok[n], fin[:, n % 2, :]).then_inc(d_res[n % 2], 16)
            for k in range(2):
                sp.wait_ge(d_res[k], 16 * (NT // 2))

        @block.gpsimd
        def _(pool):
            pool.memset(ones3[:, :], 0.0).then_inc(c_ones3, 1)
            pool.wait_ge(c_ones3, 1)
            for r in range(3):
                pool.memset(ones3[32 * r:32 * r + 1, :], 1.0).then_inc(c_ones3, 1)
                pool.wait_ge(c_ones3, 2 + r)
            pool.memset(half[:, :], -0.5).then_inc(g_half, 1)
            pool.wait_ge(g_half, 1)
            pool.memset(same_b[:, :], 0.0).then_inc(c_same, 1)
            for k in range(J):
                pool.wait_ge(c_same, 1 + k)
                v = same_b[:, :].rearrange("p (j b) -> p j b", j=J)
                pool.affine_select(out=v, in_=v, compare_op=ALU.not_equal, fill=1.0, base=-32 * k,
                                   pattern=[[0, J], [-1, 32]], channel_multiplier=1).then_inc(c_same, 1)
            pool.wait_ge(c_same, 1 + J)
            pool.memset(ident[:, :], 0.0).then_inc(c_ident, 1)
            pool.wait_ge(c_ident, 1)
            pool.affine_select(out=ident[:, :], in_=ident[:, :], compare_op=ALU.not_equal, fill=1.0, base=0,
                               pattern=[[-1, P]], channel_multiplier=1).then_inc(c_ident, 1)
            pool.wait_ge(c_ident, 2)
            pool.memset(head_mask[:, :], 1.0).then_inc(c_mask, 1)
            pool.wait_ge(c_mask, 1)
            pool.affine_select(out=head_mask[:, :], in_=head_mask[:, :], compare_op=ALU.is_ge, fill=0.0, base=0,
                               pattern=[[-DH, HC]], channel_multiplier=1).then_inc(c_mask, 1)
            pool.wait_ge(c_mask, 2)
            pool.affine_select(out=head_mask[:, :], in_=head_mask[:, :], compare_op=ALU.is_ge, fill=0.0, base=DH - 1,
                               pattern=[[DH, HC]], channel_multiplier=-1).then_inc(c_mask, 1)
            pool.wait_ge(c_mask, 3)
            for k in range(3):
                pool.memset(vblk[:, k, :, :], 0.0).then_inc(c_v, 1)
                pool.wait_ge(c_v, k + 1)
            for b in range(BT):
                for k in range(3):
                    pool.memset(vblk[32 * b:32 * b + 32, k, :, BT * DH + b:BT * DH + b + 1], 1.0).then_inc(c_v, 1)
            pool.wait_ge(c_v, 3 + 3 * BT)
            for q in range(T // G):
                pool.wait_ge(v_ms, q + 1)
                pool.tensor_tensor(rms[:, G * q:G * q + G], ms[:, G * q:G * q + G], half[:, G * q:G * q + G],
                                   ALU.pow).then_inc(g_rms, 1)

        @block.scalar
        def _(act):
            act.dma_start(bih[:, :], b_ih.rearrange("(o n) -> o n", o=1)).then_inc(d_bias, 16)
            act.dma_start(bhh[:, :], b_hh.rearrange("(o n) -> o n", o=1)).then_inc(d_bias, 16)
            for part in range(3):
                for j in range(J):
                    s = slice(XCUT[part], XCUT[part + 1])
                    act.dma_start(X[32 * j:32 * j + 32, s, :], x_jb[j][:, s, :]).then_inc(d_x[part], 16)
                if part == 0:
                    for a in range(A):
                        act.dma_start(Wih[:, a, :], rows_T(w_ih)[a]).then_inc(d_wih, 16)

            def sum_squares(t):
                act.wait_ge(v_x1, t + 1)
                if t >= 2:
                    act.wait_ge(a_ss, t - 1)
                act.activation(sq_junk[:, t % 2, :], X1[:, t, :], ACT.Square, accum_out=ssq[:, t:t + 1]).then_inc(a_ss, 1)

            for t in range(T):
                act.wait_ge(p_r, t + 1)
                if t >= 1:
                    act.wait_ge(v_rh, t)
                act.activation(r_sb[:, :], psR[t % 2][:, 0:C], ACT.Sigmoid).then_inc(a_r, 1)
                act.wait_ge(p_Z, t + 1)
                if t >= 1:
                    act.wait_ge(v_u, t)
                act.activation(z_sb[:, :], psZ, ACT.Sigmoid).then_inc(a_z, 1)
                act.wait_ge(v_npre, t + 1)
                if t >= 1:
                    act.wait_ge(v_u, t)
                act.activation(n_sb[:, :], npre, ACT.Tanh).then_inc(a_n, 1)
                if t >= 1:
                    sum_squares(t - 1)
            sum_squares(T - 1)

            def squares(n):
                act.wait_ge(p_qk, n + 1)
                if n >= 1:
                    act.wait_ge(v_ss, n)
                act.activation(sq[:, :], psQK[n % 2][:, :], ACT.Square).then_inc(a_sq, 1)
                act.activation(qk[:, n, :], psQK[n % 2][:, :], ACT.Copy).then_inc(a_qk, 1)

            def roots(k):
                act.wait_ge(v_inv, k + 1)
                act.activation(qkr[:, batch(k), :], qkinv[:, batch(k), :], ACT.Sqrt).then_inc(a_rr, 1)

            def v_operand(n):
                act.wait_ge(p_v, n + 1)
                act.wait_ge(c_v, 3 + 3 * BT)
                if n >= 3:
                    act.wait_ge(p_o, n - 2)
                for b in range(BT):
                    rows = slice(32 * b, 32 * b + 32)
                    act.activation(vblk[rows, n % 3, :, DH * b:DH * b + DH],
                                   psV[rows, 0:D].rearrange("p (h d) -> p h d", d=DH), ACT.Copy).then_inc(a_v, 1)

            def qk_T(n):
                act.wait_ge(p_t, n + 1)
                act.wait_ge(c_gk, 2)
                if n >= 2:
                    act.wait_ge(p_s, n - 1)
                if n >= 1:
                    act.wait_ge(v_kb, n)
                act.activation(kT[:, :, :], psT[:, 2 * P:4 * P].rearrange("p (a t) -> p a t", a=A), ACT.Copy).then_inc(a_k, 1)
                act.activation(qT[:, n % 2, :, :], psT[:, 0:2 * P].rearrange("p (a t) -> p a t", a=A), ACT.Copy,
                               scale=gq_p[:, 0:1]).then_inc(a_q, 1)
                act.wait_ge(a_k, n + 1)
                for h in range(HC // 2):
                    act.activation(kblk[:, n % 2, :, h, :], kT[:, :, :], ACT.Copy,
                                   scale=head_mask[:, h:h + 1]).then_inc(a_kb, 1)

            def exps(n):
                act.wait_ge(v_sm, n + 1)
                if n >= 1:
                    act.wait_ge(v_pT, n)
                act.activation(ex[:, :], sm[:, n % 3, :, :].rearrange("p h k -> p (h k)"), ACT.Exp).then_inc(a_e, 1)

            for i in range(NT + LAG_PV + 1):
                if i < NT:
                    squares(i)
                if i % NB == NB - 1 and i < NT:
                    roots(i // NB)
                if 0 <= i - LAG_PV < NT:
                    exps(i - LAG_PV)
                if 0 <= i - LAG_T < NT:
                    qk_T(i - LAG_T)
                if 0 <= i - LAG_S < NT:
                    v_operand(i - LAG_S)

        @block.vector
        def _(dve):
            dve.memset(warm[:, :], 0.0).then_inc(c_warm, 1)
            dve.wait_ge(d_bias, 32)
            dve.tensor_tensor(bsum[:, 0, :], bih[:, 0:D], bhh[:, 0:D], ALU.add).then_inc(c_bias, 1)
            dve.tensor_tensor(bsum[:, 3, :], bih[:, D:2 * D], bhh[:, D:2 * D], ALU.add).then_inc(c_bias, 1)
            dve.tensor_copy(bsum[:, 2, :], bhh[:, 2 * D:3 * D]).then_inc(c_bias, 1)
            dve.tensor_copy(bsum[:, 1, :], bih[:, 2 * D:3 * D]).then_inc(c_bias, 1)
            dve.wait_ge(c_bias, 4)
            dve.tensor_copy(bhi[:, :, :], bsum[:, :, :]).then_inc(c_bias, 1)
            dve.wait_ge(c_bias, 5)
            dve.tensor_tensor(blo[:, :, :], bsum[:, :, :], bhi[:, :, :], ALU.subtract).then_inc(c_bias, 1)
            dve.wait_ge(c_bias, 6)
            dve.tensor_copy(bmid[:, :, :], blo[:, :, :]).then_inc(c_bias, 1)
            dve.memset(bias3[:, :, :], 0.0).then_inc(c_bias, 1)
            dve.wait_ge(c_bias, 8)
            dve.tensor_copy(bias3[0:1, :, :], bhi[:, :, :]).then_inc(c_bias, 1)
            dve.tensor_copy(bias3[32:33, :, :], bmid[:, :, :]).then_inc(c_bias, 1)
            dve.tensor_tensor(bias3[64:65, :, :], blo[:, :, :], bmid[:, :, :], ALU.subtract).then_inc(c_bias, 1)

            def part_of(t):
                return 0 if t < XCUT[1] else 1 if t < XCUT[2] else 2

            def x_transpose(t):
                dve.wait_ge(d_x[part_of(t)], 16 * J)
                if t >= 2:
                    dve.wait_ge(p_Z, t - 1)
                dve.transpose(xT[:, t % 2, :, :].rearrange("p a b -> p (a b)"), X[:, t, :]).then_inc(v_xT, 1)

            dve.wait_ge(d_cond, 16 * J)
            dve.transpose(hT[:, 0, :, :].rearrange("p a b -> p (a b)"), H[:, 0, :]).then_inc(v_hT, 1)
            dve.transpose(condT[:, :, :].rearrange("p a b -> p (a b)"), H[:, 0, :]).then_inc(c_condT, 1)
            x_transpose(0)
            x_transpose(1)
            def residual(t):
                dve.wait_ge(v_h, t + 1)
                dve.tensor_tensor(X1[:, t, :], X[:, t, :], H[:, t + 1, :], ALU.add).then_inc(v_x1, 1)

            def mean_square(q):
                dve.wait_ge(p_ss, q + 1)
                dve.tensor_scalar(ms[:, G * q:G * q + G], psM[:, G * q:G * q + G], 1.0 / D, EPS,
                                  ALU.mult, ALU.add).then_inc(v_ms, 1)

            def norm(t):
                dve.wait_ge(g_rms, t // G + 1)
                dve.wait_ge(v_x1, t + 1)
                dve.wait_ge(v_gs, 3)
                dve.scalar_tensor_tensor(out=y0[:, :], in0=X1[:, t, :], scalar=rms[:, t:t + 1], in1=gain[:, :],
                                         op0=ALU.mult, op1=ALU.mult).then_inc(v_y0, 1)
                dve.wait_ge(v_y0, t + 1)
                dve.tensor_tensor(y[:, :], y0[:, :], shift[:, :], ALU.add).then_inc(v_y, 1)
                dve.wait_ge(v_y, t + 1)
                dve.transpose(yT[:, :, :, t], y[:, :]).then_inc(v_yT, 1)

            def conditioning():
                dve.wait_ge(d_emb, 16 * (A + 2 * J))
                dve.wait_ge(p_E, 1)
                dve.scalar_tensor_tensor(out=gain[:, :], in0=psE[:, 0:C], scalar=1.0, in1=bemb_jb[:, 0, :],
                                         op0=ALU.add, op1=ALU.add).then_inc(v_gs, 1)
                dve.tensor_tensor(shift[:, :], psE[:, C:2 * C], bemb_jb[:, 1, :], ALU.add).then_inc(v_gs, 1)
                dve.wait_ge(v_gs, 1)
                dve.tensor_tensor(gain[:, :], gain[:, :], gnorm_jb[:, :], ALU.mult).then_inc(v_gs, 1)

            LAG = G + 2
            for t in range(T):
                h_new = H[:, t + 1, :]
                dve.wait_ge(a_r, t + 1)
                dve.wait_ge(p_hn, t + 1)
                dve.tensor_tensor(rh[:, :], psN, r_sb[:, :], ALU.mult).then_inc(v_rh, 1)
                dve.wait_ge(v_rh, t + 1)
                dve.tensor_tensor(npre, psR[t % 2][:, C:2 * C], rh[:, :], ALU.add).then_inc(v_npre, 1)
                dve.wait_ge(a_z, t + 1)
                dve.tensor_tensor(zh[:, :], z_sb[:, :], H[:, t, :], ALU.mult).then_inc(v_zh, 1)
                dve.wait_ge(a_n, t + 1)
                dve.scalar_tensor_tensor(out=u_sb[:, :], in0=z_sb[:, :], scalar=1.0, in1=n_sb[:, :],
                                         op0=ALU.subtract, op1=ALU.mult).then_inc(v_u, 1)
                dve.wait_ge(v_u, t + 1)
                dve.tensor_tensor(h_new, zh[:, :], u_sb[:, :], ALU.subtract).then_inc(v_h, 1)
                dve.wait_ge(v_h, t + 1)
                if t < T - 1:
                    dve.transpose(hT[:, (t + 1) % 2, :, :].rearrange("p a b -> p (a b)"), h_new).then_inc(v_hT, 1)
                residual(t)
                if t + 2 < T:
                    x_transpose(t + 2)
                if t == EMB_STEP:
                    conditioning()
                if t % G == 1 and t > G:
                    mean_square(t // G - 1)
                if t >= LAG + 1:
                    norm(t - LAG - 1)
            mean_square(T // G - 1)
            for t in range(T - LAG - 1, T):
                norm(t)

            dve.wait_ge(d_gqk, 16 * 2 * HC)
            dve.wait_ge(c_mask, 3)
            dve.wait_ge(c_ident, 2)
            dve.tensor_scalar(gq_p[:, :], gq_p[:, :], DH ** -0.5, None, ALU.mult).then_inc(c_gk, 1)
            dve.tensor_scalar(head_mask[:, :], head_mask[:, :], gk_p[:, 0:1], None, ALU.mult).then_inc(c_gk, 1)
            dve.wait_ge(d_out_w, 16 * A)
            for a in range(A):
                dve.tensor_tensor(Wout[:, a, P * a:P * a + P], Wout[:, a, P * a:P * a + P], ident[:, :],
                                  ALU.add).then_inc(c_wout, 1)

            def qk_sums(n):
                dve.wait_ge(a_sq, n + 1)
                dve.tensor_reduce(qkss[:, n, :], sq[:, :].rearrange("p (h d) -> p h d", d=DH), AX.X, ALU.add).then_inc(v_ss, 1)

            def inverses(k):
                dve.wait_ge(v_ss, NB * k + NB)
                dve.tensor_scalar(qkms[:, batch(k), :], qkss[:, batch(k), :], 1.0 / DH, EPS, ALU.mult, ALU.add).then_inc(v_ms2, 1)
                dve.wait_ge(v_ms2, k + 1)
                dve.reciprocal(qkinv[:, batch(k), :], qkms[:, batch(k), :]).then_inc(v_inv, 1)

            def qk_scale(n):
                dve.wait_ge(a_rr, n // NB + 1)
                dve.wait_ge(a_qk, n + 1)
                if n >= 2:
                    dve.wait_ge(p_t, n - 1)
                dve.tensor_tensor(qkn[:, n % 2, :].rearrange("p (h d) -> p h d", d=DH),
                                  qk[:, n, :].rearrange("p (h d) -> p h d", d=DH),
                                  qkr[:, n, :].unsqueeze(2).broadcast_to([P, 2 * HEADS, DH]), ALU.mult).then_inc(v_qkn, 1)

            def k_blocks(n):
                dve.wait_ge(a_k, n + 1)
                dve.wait_ge(c_gk, 2)
                if n >= 2:
                    dve.wait_ge(p_s, n - 1)
                for h in range(HC // 2, HC):
                    last = dve.tensor_scalar(kblk[:, n % 2, :, h, :], kT[:, :, :], head_mask[:, h:h + 1], None, ALU.mult)
                last.then_inc(v_kb, 1)

            def softmax_shift(n):
                S = psS[n % 2][:, :].rearrange("p (h k) -> p h k", k=T)
                dve.wait_ge(p_s, n + 1)
                dve.tensor_reduce(mx[:, :], S, AX.X, ALU.max).then_inc(v_mx, 1)
                dve.wait_ge(v_mx, n + 1)
                if n >= 3:
                    dve.wait_ge(a_e, n - 2)
                dve.tensor_tensor(sm[:, n % 3, :, :], S, mx[:, :].unsqueeze(2).broadcast_to([P, HEADS, T]),
                                  ALU.subtract).then_inc(v_sm, 1)

            def p_transpose(n):
                dve.wait_ge(a_e, n + 1)
                if n >= 2:
                    dve.wait_ge(p_o, n - 1)
                dve.transpose(pT[:, n % 2, :], ex[:, :]).then_inc(v_pT, 1)

            def o_norm(n):
                O = psO[:, 0:4 * VW].rearrange("p (c w) -> p c w", w=VW)
                dve.wait_ge(p_o, n + 1)
                dve.reciprocal(rden[:, :, :], O[:, :, BT * DH:VW]).then_inc(v_rd, 1)
                dve.wait_ge(v_rd, n + 1)
                for s in range(4):
                    last = dve.tensor_tensor(on[:, :, s // 2, s % 2, :],
                                             O[:, s, 0:BT * DH].rearrange("p (b d) -> p b d", d=DH),
                                             rden[:, s, :].unsqueeze(2).broadcast_to([P, BT, DH]), ALU.mult)
                last.then_inc(v_on, 1)
                dve.wait_ge(v_on, n + 1)
                if n >= 2:
                    dve.wait_ge(p_y, n - 1)
                for a in range(A):
                    last = dve.transpose(oT[:, n % 2, a, :, :],
                                         on[:, :, a, :, :].rearrange("p b s d -> p b (s d)"))
                last.then_inc(v_oT, 1)

            def last_residual(n):
                dve.wait_ge(p_y, n + 1)
                dve.wait_ge(d_x1ld, 16)
                if n >= 2:
                    dve.wait_ge(d_res[n % 2], 16 * (n // 2))
                dve.tensor_tensor(fin[:, n % 2, :], psY[:, 0:D], x1tok[:, n, :], ALU.add).then_inc(v_fin, 1)

            for i in range(NT + LAG_Y + 1):
                if i < NT:
                    qk_sums(i)
                if i % NB == NB - 1 and i < NT:
                    inverses(i // NB)
                if 0 <= i - LAG_S < NT:
                    softmax_shift(i - LAG_S)
                if 0 <= i - LAG_T + 1 < NT:
                    qk_scale(i - LAG_T + 1)
                if 0 <= i - LAG_T < NT:
                    k_blocks(i - LAG_T)
                if 0 <= i - LAG_PV < NT:
                    p_transpose(i - LAG_PV)
                if 0 <= i - LAG_PV - 1 < NT:
                    o_norm(i - LAG_PV - 1)
                if 0 <= i - LAG_Y < NT:
                    last_residual(i - LAG_Y)

        @block.tensor
        def _(pe):
            wih = Wih[:, :, :].rearrange("p a (g n) -> p a g n", g=3)
            whh = Whh[:, :, :].rearrange("p a (g n) -> p a g n", g=3)
            wemb = Wemb[:, :, :].rearrange("p a (g n) -> p a g n", g=2)

            def x_gates(t):
                def bias(ps, first, count):
                    for j in range(J):
                        rows = slice(32 * j, 32 * j + 32)
                        pe.matmul(ps[rows, :].rearrange("p (g c) -> p g c", g=count), ones3[:, :],
                                  bias3[:, first:first + count, C * j:C * j + C], start=True, stop=False,
                                  skip_group_check=True)

                def products(ps, gates):
                    for a in range(A):
                        for j in range(J):
                            rows = slice(32 * j, 32 * j + 32)
                            pe.matmul(ps[rows, :].rearrange("p (g c) -> p g c", c=C), xT[:, t % 2, a, :],
                                      wih[:, a, gates, C * j:C * j + C], start=False, stop=False, skip_group_check=True)

                pe.wait_ge(v_xT, t + 1)
                if t >= 2:
                    pe.wait_ge(v_npre, t - 1)
                bias(psR[t % 2], 0, 2)
                products(psR[t % 2], slice(0, 3, 2))
                if t >= 1:
                    pe.wait_ge(v_rh, t)
                    pe.wait_ge(a_z, t)
                bias(psN, 2, 1)
                bias(psZ, 3, 1)
                products(psZ, slice(1, 2))

            def h_gates(t):
                pe.wait_ge(v_hT, t + 1)
                for ps, gate, done in ((psR[t % 2][:, 0:C], 0, p_r), (psN, 2, p_hn), (psZ, 1, p_Z)):
                    for a in range(A):
                        for j in range(J):
                            rows = slice(32 * j, 32 * j + 32)
                            last = pe.matmul(ps[rows, :], hT[:, t % 2, a, :], whh[:, a, gate, C * j:C * j + C],
                                             start=False, stop=(a == A - 1), skip_group_check=True)
                    last.then_inc(done, 1)

            pe.wait_ge(c_warm, 1)
            for k in range(WARM):
                pe.matmul(psY[:, :], warm[:, 0:P], warm[:, :], start=True, stop=True, skip_group_check=True)
            pe.wait_ge(c_ones3, 4)
            pe.wait_ge(c_bias, 11)
            pe.wait_ge(d_wih, 16 * A)
            x_gates(0)
            pe.wait_ge(d_whh, 16 * A)
            for t in range(T):
                h_gates(t)
                if t == EMB_STEP:
                    pe.wait_ge(c_condT, 1)
                    pe.wait_ge(d_emb, 16 * (A + 2 * J))
                    for a in range(A):
                        for j in range(J):
                            rows = slice(32 * j, 32 * j + 32)
                            last = pe.matmul(psE[rows, :].rearrange("p (g c) -> p g c", g=2), condT[:, a, :],
                                             wemb[:, a, :, C * j:C * j + C], start=(a == 0), stop=(a == A - 1),
                                             skip_group_check=True)
                    last.then_inc(p_E, 1)
                if t + 1 < T:
                    x_gates(t + 1)
                if t % G == 0 and t > 0:
                    q = t // G - 1
                    if q == 0:
                        pe.wait_ge(c_same, 1 + J)
                    pe.wait_ge(a_ss, G * q + G)
                    if q >= 1:
                        pe.wait_ge(v_ms, q)
                    pe.matmul(psM[:, G * q:G * q + G], same_b[:, :], ssq[:, G * q:G * q + G],
                              start=True, stop=True, skip_group_check=True).then_inc(p_ss, 1)
            q = T // G - 1
            pe.wait_ge(a_ss, T)
            pe.wait_ge(v_ms, q)
            pe.matmul(psM[:, G * q:G * q + G], same_b[:, :], ssq[:, G * q:G * q + G],
                      start=True, stop=True, skip_group_check=True).then_inc(p_ss, 1)

            def project(n):
                if n == 0:
                    pe.wait_ge(d_qkv, 16 * A)
                    pe.wait_ge(v_yT, T)
                if n >= 2:
                    pe.wait_ge(a_qk, n - 1)
                for a in range(A):
                    toks = yT[:, a, BT * n:BT * n + BT, :].rearrange("p b t -> p (b t)")
                    last = pe.matmul(psQK[n % 2][:, :], toks, Wqkv[:, a, 0:2 * D], start=(a == 0), stop=(a == A - 1))
                last.then_inc(p_qk, 1)

            def project_v(n):
                if n >= 1:
                    pe.wait_ge(a_v, BT * n)
                for a in range(A):
                    toks = yT[:, a, BT * n:BT * n + BT, :].rearrange("p b t -> p (b t)")
                    last = pe.matmul(psV[:, 0:D], toks, Wqkv[:, a, 2 * D:3 * D], start=(a == 0), stop=(a == A - 1))
                last.then_inc(p_v, 1)

            def transposes(n):
                pe.wait_ge(v_qkn, n + 1)
                if n >= 1:
                    pe.wait_ge(a_q, n)
                for c in range(4):
                    last = pe.transpose(psT[:, P * c:P * c + P], qkn[:, n % 2, P * c:P * c + P], ident[:, :])
                last.then_inc(p_t, 1)

            def scores(n):
                pe.wait_ge(a_q, n + 1)
                pe.wait_ge(a_kb, (HC // 2) * (n + 1))
                pe.wait_ge(v_kb, n + 1)
                if n >= 2:
                    pe.wait_ge(v_sm, n - 1)
                for a in range(A):
                    for b in range(BT):
                        cols = slice(32 * b, 32 * b + 32)
                        last = pe.matmul(psS[n % 2][cols, D * a:D * a + D].rearrange("p (h k) -> p h k", k=T),
                                         qT[:, n % 2, a, cols], kblk[:, n % 2, a, :, cols], start=True, stop=True)
                last.then_inc(p_s, 1)

            def attend(n):
                pe.wait_ge(v_pT, n + 1)
                pe.wait_ge(a_v, BT * (n + 1))
                if n >= 1:
                    pe.wait_ge(v_on, n)
                for cs in range(4):
                    for g in range(4):
                        h = 8 * (cs // 2) + 2 * g + cs % 2
                        last = pe.matmul(psO[32 * g:32 * g + 32, VW * cs:VW * cs + VW], pT[:, n % 2, T * h:T * h + T],
                                         vblk[:, n % 3, h, :], start=True, stop=True)
                last.then_inc(p_o, 1)

            def out_project(n):
                pe.wait_ge(v_oT, n + 1)
                pe.wait_ge(c_wout, A)
                if n >= 1:
                    pe.wait_ge(v_fin, n)
                for a in range(A):
                    last = pe.matmul(psY[:, 0:D], oT[:, n % 2, a, :, :].rearrange("p b t -> p (b t)"), Wout[:, a, :],
                                     start=(a == 0), stop=(a == A - 1))
                last.then_inc(p_y, 1)

            pe.wait_ge(c_ident, 2)
            for i in range(NT + LAG_Y + 1):
                if i < NT:
                    project(i)
                if 0 <= i - LAG_S < NT:
                    scores(i - LAG_S)
                    project_v(i - LAG_S)
                if 0 <= i - LAG_T < NT:
                    transposes(i - LAG_T)
                if 0 <= i - LAG_PV < NT:
                    attend(i - LAG_PV)
                if 0 <= i - LAG_Y < NT:
                    out_project(i - LAG_Y)


_INS = ["x", "cond_2048", "L0_cond_W_ih", "L0_cond_W_hh", "L0_cond_b_ih", "L0_cond_b_hh", "L1_cond_W_emb",
        "L1_cond_b_emb", "L1_cond_g_norm", "L1_cond_W_qkv", "L1_cond_g_q", "L1_cond_g_k", "L1_cond_W_out"]


def kernel(**inputs):
    import numpy as _np
    import concourse.bacc as _bacc
    from concourse import mybir as _mybir
    from concourse.bass_utils import run_bass_kernel_spmd as _run

    nc = _bacc.Bacc("TRN2", target_bir_lowering=False, num_devices=1)
    arrays, args = {}, []
    for name in _INS:
        a = _np.ascontiguousarray(inputs[name])
        arrays[f"in_{name}_dram"] = a
        args.append(nc.dram_tensor(f"in_{name}_dram", a.shape, _mybir.dt.from_np(a.dtype), kind="ExternalInput").ap())
    args.append(nc.dram_tensor("out_0_dram", (B, T, D), F32, kind="ExternalOutput").ap())
    args.append(nc.dram_tensor("x1_scratch", (B, T, D), F32, kind="Internal").ap())
    build(nc, *args)
    r = _run(nc, [arrays], core_ids=[0])
    return r.results[0]["out_0_dram"]
```

```python
from contextlib import ExitStack

import concourse.bass as bass
from concourse import mybir

F32 = mybir.dt.float32
BF16 = mybir.dt.bfloat16
F32R = mybir.dt.float32r
ALU = mybir.AluOpType
ACT = mybir.ActivationFunctionType
AX = mybir.AxisListType

P = 128
B, T, D = 32, 32, 256
J = 4
C = D // J
A = D // P
G = 4
HEADS, DH = 16, 16
NT = B * T // P
BT = P // T
HC = P // DH
NB = 4
LAG_S, LAG_P, LAG_Y = 1, 2, 3
turns = range(NT + LAG_Y)
VW = BT * DH + BT
EPS = 1e-6
EMB_STEP = 3
WARM = 7
FILL_0 = 2
FILL_TURNS = 3
FILL = 3
WARM_END = 4
WARM_NORM = 9


def due(i, lag):
    return 0 <= i - lag < NT


def batch(k):
    return slice(NB * k, NB * k + NB)


def build(nc, x, cond, w_ih, w_hh, b_ih, b_hh, w_emb, b_emb, g_norm, w_qkv, g_q, g_k, w_out, out, x1_dram):
    with ExitStack() as ctx:
        def sb(name, shape, dt=F32):
            return ctx.enter_context(nc.sbuf_tensor(name, shape, dt))

        def sem(name):
            return ctx.enter_context(nc.semaphore(name))

        X = sb("X", [P, T, C])
        Wih = sb("Wih", [P, A, 3 * D])
        Whh = sb("Whh", [P, A, 3 * D])
        Wemb = sb("Wemb", [P, A, 2 * D])
        Wqkv = sb("Wqkv", [P, A, 3 * D])
        Wout = sb("Wout", [P, A, D])
        bih = sb("bih", [J, 3, C])
        bhh = sb("bhh", [J, 3, C])
        bemb_jb = sb("bemb_jb", [P, 2, C])
        gnorm_jb = sb("gnorm_jb", [P, C])
        gq_p = sb("gq_p", [P, 1])
        gk_p = sb("gk_p", [P, 1])
        ident = sb("ident", [P, P])
        same_b = sb("same_b", [P, P])
        head_rows = sb("head_rows", [P, 2, 4])
        row_mask = sb("row_mask", [P, 4])
        to_jb_f = sb("to_jb_f", [3 * J, P])
        to_jb = sb("to_jb", [3 * J, P], BF16)
        bias3 = sb("bias3", [3 * J, 4, C], BF16)
        bsum = sb("bsum", [J, 4, C])
        bhi = sb("bhi", [J, 4, C], BF16)
        blo = sb("blo", [J, 4, C])
        bmid = sb("bmid", [J, 4, C], BF16)
        blow = sb("blow", [J, 4, C], BF16)
        warm = sb("warm", [P, 512])
        H = sb("H", [P, T + 1, C])
        hT = sb("hT", [P, 2, A, 32])
        condT = sb("condT", [P, A, 32])
        xT = sb("xT", [P, 2, A, 32])
        r_sb = sb("r_sb", [P, C])
        z_sb = sb("z_sb", [P, C])
        n_sb = sb("n_sb", [P, C])
        rh = sb("rh", [P, C])
        zh = sb("zh", [P, C])
        u_sb = sb("u_sb", [P, C])
        X1 = sb("X1", [P, T, C])
        sq_junk = sb("sq_junk", [P, 2, C])
        ssq = sb("ssq", [P, T])
        ms = sb("ms", [P, T])
        half = sb("half", [P, T])
        rms = sb("rms", [P, T])
        gain = sb("gain", [P, C])
        shift = sb("shift", [P, C])
        y0 = sb("y0", [P, G, C])
        y = sb("y", [P, G, C])
        yT = sb("yT", [P, A, B, T])
        y_hi = sb("y_hi", [P, A, B, T], F32R)
        y_lo = sb("y_lo", [P, A, B, T], F32R)
        w_hi = sb("w_hi", [P, A, 3 * D], F32R)
        w_lo = sb("w_lo", [P, A, 3 * D], F32R)
        x1tok = sb("x1tok", [P, NT, D])
        sq = sb("sq", [P, 2 * D])
        qk = sb("qk", [P, NT, 2 * D])
        qkss = sb("qkss", [P, NT, 2 * HEADS])
        qkms = sb("qkms", [P, NT, 2 * HEADS])
        qkinv = sb("qkinv", [P, NT, 2 * HEADS])
        qkr = sb("qkr", [P, NT, 2 * HEADS])
        qkn = sb("qkn", [P, 2, 2 * D])
        qT = sb("qT", [P, 2, A, P])
        k4 = sb("k4", [P, 2, A, 4, P])
        vblk = sb("vblk", [P, NT, HEADS, VW])
        v_counts = sb("v_counts", [P, BT])
        mx = sb("mx", [P, 2, 2, 8])
        sm = sb("sm", [P, 2, 2, 8, T])
        ex = sb("ex", [P, HEADS * T])
        pT = sb("pT", [P, 2, HEADS * T])
        rden = sb("rden", [P, 4, BT])
        o_n = sb("o_n", [P, BT, HEADS // 4, DH])
        oT = sb("oT", [P, 2, A, BT, T])
        y_out = sb("y_out", [P, 2, D])
        fin = sb("fin", [P, 2, D])

        psS = ctx.enter_context(nc.psum_tensor("psS", [P, 2, 2, 512], F32))
        banks = [psS[:, i // 2, i % 2, :] for i in range(4)]
        banks += [ctx.enter_context(nc.psum_tensor(f"bank{i}", [P, 512], F32))[:, :] for i in range(4, 8)]
        psR = [banks[5][:, 0:C], banks[6][:, 0:C]]
        psN = [banks[0][:, 0:2 * C], banks[1][:, 0:2 * C]]
        psZ = [banks[2][:, 0:C], banks[3][:, 0:C]]
        npre = banks[4][:, 0:C]
        psE = banks[7][:, 0:2 * C]
        psM = banks[7][:, 2 * C:2 * C + T]
        psQK = [banks[4], banks[5], banks[1]]
        psV = [banks[3], banks[2]]
        psT = [banks[6], banks[7]]
        psO = banks[4]
        psY = banks[5]

        d_cond, d_whh, d_wih, d_bias = sem("d_cond"), sem("d_whh"), sem("d_wih"), sem("d_bias")
        d_x = [sem(f"d_x{i}") for i in range(3)]
        d_emb, d_qkv, d_out_w, d_gqk, d_bias3 = sem("d_emb"), sem("d_qkv"), sem("d_out_w"), sem("d_gqk"), sem("d_bias3")
        a_y, g_fin = sem("a_y"), sem("g_fin")
        d_x1st, d_x1ld = sem("d_x1st"), sem("d_x1ld")
        d_res = [sem("d_res0"), sem("d_res1")]
        c_warm, c_condT, a_first, c_half, a_exp_in = sem("c_warm"), sem("c_condT"), sem("a_first"), sem("c_half"), sem("a_exp_in")
        c_same, c_ident, c_mask, c_to_jb, c_bias = (sem(s) for s in ("c_same", "c_ident", "c_mask", "c_to_jb", "c_bias"))
        c_gk, c_wout, c_v, c_vc = sem("c_gk"), sem("c_wout"), sem("c_v"), sem("c_vc")
        p_r, p_hn, p_Z = sem("p_r"), sem("p_hn"), sem("p_Z")
        a_r, a_z, a_n = sem("a_r"), sem("a_z"), sem("a_n")
        v_rh, v_npre, v_zh, v_u, v_h, v_hT, v_xT = (sem(s) for s in (
            "v_rh", "v_npre", "v_zh", "v_u", "v_h", "v_hT", "v_xT"))
        g_whi, g_wlo, g_yhi, g_ylo, a_yhi, v_ylo, v_x1, a_ss, p_ss, v_ms, g_half, g_rms, v_y0, v_y, v_yT = (sem(s) for s in (
            "g_whi", "g_wlo", "g_yhi", "g_ylo", "a_yhi", "v_ylo", "v_x1", "a_ss", "p_ss", "v_ms", "g_half", "g_rms", "v_y0", "v_y", "v_yT"))
        p_E, v_gs = sem("p_E"), sem("v_gs")
        p_qk, p_v, p_t, p_s, p_o, p_y = (sem(s) for s in ("p_qk", "p_v", "p_t", "p_s", "p_o", "p_y"))
        a_sq, v_qk, a_rr, a_q, a_k, a_v, a_e = (sem(s) for s in (
            "a_sq", "v_qk", "a_rr", "a_q", "a_k", "a_v", "a_e"))
        g_qkn, v_ms2, v_inv, v_ss, v_mx, v_sm, v_pT, v_rd, v_on, v_oT, v_fin = (sem(s) for s in (
            "g_qkn", "v_ms2", "v_inv", "v_ss", "v_mx", "v_sm", "v_pT", "v_rd", "v_on", "v_oT", "v_fin"))

        x_jb = x.rearrange("b t (j c) -> j b t c", j=J)
        x1_jb = x1_dram.rearrange("b t (j c) -> j b t c", j=J)
        cond_jb = cond.rearrange("b (j c) -> j b c", j=J)
        x1_tok = x1_dram.rearrange("(n b) t d -> (b t) n d", n=NT)
        out_tok = out.rearrange("(n b) t d -> n (b t) d", n=NT)

        def rows_T(w):
            return w.rearrange("(j a i) n -> a j i n", a=A, i=32)

        XCUT = [0, 2, 10, T]
        block = ctx.enter_context(nc.Block())

        @block.sync
        def _(sp):
            sp.dma_start(H[:, 0, :], cond_jb).then_inc(d_cond, 16)
            for t in range(XCUT[1]):
                sp.dma_start(X[:, t, :], x_jb[:, :, t, :]).then_inc(d_x[0], 16)
            for a in range(A):
                sp.dma_start(Wih[:, a, :], rows_T(w_ih)[a]).then_inc(d_wih, 16)
            for part in range(1, 3):
                for j in range(J):
                    s = slice(XCUT[part], XCUT[part + 1])
                    sp.dma_start(X[32 * j:32 * j + 32, s, :], x_jb[j][:, s, :]).then_inc(d_x[part], 16)
            for a in range(A):
                sp.dma_start(Wemb[:, a, :], rows_T(w_emb)[a]).then_inc(d_emb, 16)
            sp.dma_start(gnorm_jb[:, :], g_norm.rearrange("(j o c) -> j o c", j=J, o=1).broadcast_to([J, B, C])).then_inc(d_emb, 16)
            for s in range(2):
                sp.dma_start(bemb_jb[:, s, :],
                             b_emb.rearrange("(s j o c) -> s j o c", j=J, s=2, o=1)[s].broadcast_to([J, B, C])).then_inc(d_emb, 16)
            for a in range(A):
                sp.dma_start(Wqkv[:, a, :], rows_T(w_qkv)[a]).then_inc(d_qkv, 16)
                sp.dma_start(Wout[:, a, :], w_out[P * a:P * a + P, :]).then_inc(d_out_w, 16)
            for g_dram, g_sb in ((g_q, gq_p), (g_k, gk_p)):
                sp.dma_start(g_sb[:, :], g_dram.rearrange("(u d o) -> u d o", u=1, o=1).broadcast_to([HC, DH, 1])).then_inc(d_gqk, 16)
            for q in range(T // 8):
                sp.wait_ge(v_x1, 8 * q + 8)
                for j in range(J):
                    sp.dma_start(x1_jb[j][:, 8 * q:8 * q + 8, :], X1[32 * j:32 * j + 32, 8 * q:8 * q + 8, :]).then_inc(d_x1st, 16)
            sp.wait_ge(d_x1st, 16 * J * (T // 8))
            sp.dma_start(x1tok[:, :, :], x1_tok).then_inc(d_x1ld, 16)
            for n in range(NT):
                if n < NT - 1:
                    sp.wait_ge(g_fin, n + 1)
                else:
                    sp.wait_ge(v_fin, 1)
                sp.dma_start(out_tok[n], fin[:, n % 2, :]).then_inc(d_res[n % 2], 16)
            for k in range(2):
                sp.wait_ge(d_res[k], 16 * (NT // 2))

        @block.gpsimd
        def _(pool):
            pool.memset(to_jb_f[:, :], 0.0).then_inc(c_to_jb, 1)
            for k in range(3):
                pool.wait_ge(c_to_jb, 1 + k)
                v = to_jb_f[:, :].rearrange("p (j b) -> p j b", j=J)
                pool.affine_select(out=v, in_=v, compare_op=ALU.not_equal, fill=1.0, base=-J * k,
                                   pattern=[[-1, J], [0, 32]], channel_multiplier=1).then_inc(c_to_jb, 1)
            pool.wait_ge(c_to_jb, 4)
            pool.tensor_copy(to_jb[:, :], to_jb_f[:, :]).then_inc(c_to_jb, 1)
            pool.wait_ge(c_to_jb, 5)
            pool.memset(half[:, :], -0.5).then_inc(g_half, 1)
            pool.wait_ge(g_half, 1)
            pool.memset(same_b[:, :], 0.0).then_inc(c_same, 1)
            for k in range(J):
                pool.wait_ge(c_same, 1 + k)
                v = same_b[:, :].rearrange("p (j b) -> p j b", j=J)
                pool.affine_select(out=v, in_=v, compare_op=ALU.not_equal, fill=1.0, base=-32 * k,
                                   pattern=[[0, J], [-1, 32]], channel_multiplier=1).then_inc(c_same, 1)
            pool.wait_ge(c_same, 1 + J)
            pool.memset(ident[:, :], 0.0).then_inc(c_ident, 1)
            pool.wait_ge(c_ident, 1)
            pool.affine_select(out=ident[:, :], in_=ident[:, :], compare_op=ALU.not_equal, fill=1.0, base=0,
                               pattern=[[-1, P]], channel_multiplier=1).then_inc(c_ident, 1)
            pool.wait_ge(c_ident, 2)
            pool.memset(head_rows[:, :, :], 1.0).then_inc(c_mask, 1)
            pool.wait_ge(c_mask, 1)
            pool.affine_select(out=head_rows[:, :, :], in_=head_rows[:, :, :], compare_op=ALU.is_ge, fill=0.0, base=0,
                               pattern=[[-4 * DH, 2], [-DH, 4]], channel_multiplier=1).then_inc(c_mask, 1)
            pool.wait_ge(c_mask, 2)
            pool.affine_select(out=head_rows[:, :, :], in_=head_rows[:, :, :], compare_op=ALU.is_ge, fill=0.0, base=DH - 1,
                               pattern=[[4 * DH, 2], [DH, 4]], channel_multiplier=-1).then_inc(c_mask, 1)
            pool.wait_ge(c_mask, 3)
            for b in range(BT):
                pool.memset(v_counts[32 * b:32 * b + 32, :], 0.0).then_inc(c_vc, 1)
                pool.wait_ge(c_vc, 2 * b + 1)
                pool.memset(v_counts[32 * b:32 * b + 32, b:b + 1], 1.0).then_inc(c_vc, 1)
                pool.wait_ge(c_vc, 2 * b + 2)
            def v_zeros(k):
                pool.memset(vblk[:, k, :, :], 0.0).then_inc(c_v, 1)
                pool.wait_ge(c_v, 2 * k + 1)
                v = vblk[:, k, :, BT * DH:VW]
                pool.tensor_copy(v, v_counts[:, :].unsqueeze(1).broadcast_to([P, HEADS, BT])).then_inc(c_v, 1)
                pool.wait_ge(c_v, 2 * k + 2)

            pool.wait_ge(d_qkv, 16 * A)
            for a in range(A):
                pool.tensor_copy(w_hi[:, a, :], Wqkv[:, a, :]).then_inc(g_whi, 1)
                pool.wait_ge(g_whi, a + 1)
                pool.tensor_tensor(w_lo[:, a, :], Wqkv[:, a, :], w_hi[:, a, :], ALU.subtract).then_inc(g_wlo, 1)

            def y_parts(q):
                s = slice(G * q, G * q + G)
                pool.wait_ge(v_yT, G * q + G)
                pool.tensor_copy(y_hi[:, :, :, s], yT[:, :, :, s]).then_inc(g_yhi, 1)
                pool.wait_ge(g_yhi, q + 1)
                pool.tensor_tensor(y_lo[:, :, :, s], yT[:, :, :, s], y_hi[:, :, :, s], ALU.subtract).then_inc(g_ylo, 1)

            for q in range(T // G):
                if 2 * q < NT:
                    v_zeros(2 * q)
                    v_zeros(2 * q + 1)
                if q >= 2:
                    y_parts(q - 2)
                pool.wait_ge(v_ms, q + 1)
                pool.tensor_tensor(rms[:, G * q:G * q + G], ms[:, G * q:G * q + G], half[:, G * q:G * q + G],
                                   ALU.pow).then_inc(g_rms, 1)
            y_parts(T // G - 2)
            def qk_scale(n):
                pool.wait_ge(a_rr, n // NB + 1)
                pool.wait_ge(v_qk, n + 1)
                if n >= 2:
                    pool.wait_ge(p_t, n - 1)
                pool.tensor_tensor(qkn[:, n % 2, :].rearrange("p (h d) -> p h d", d=DH),
                                   qk[:, n, :].rearrange("p (h d) -> p h d", d=DH),
                                   qkr[:, n, :].unsqueeze(2).broadcast_to([P, 2 * HEADS, DH]), ALU.mult).then_inc(g_qkn, 1)

            def last_residual(n):
                pool.wait_ge(a_y, n + 1)
                if n == 0:
                    pool.wait_ge(d_x1ld, 16)
                if n >= 2:
                    pool.wait_ge(d_res[n % 2], 16 * (n // 2))
                pool.tensor_tensor(fin[:, n % 2, :], y_out[:, n % 2, :], x1tok[:, n, :], ALU.add).then_inc(g_fin, 1)

            qk_scale(0)
            qk_scale(1)
            for i in turns:
                if i + 2 < NT:
                    qk_scale(i + 2)
                if due(i, LAG_Y) and i - LAG_Y < NT - 1:
                    last_residual(i - LAG_Y)

        @block.scalar
        def _(act):
            act.dma_start(bih[:, :, :], b_ih.rearrange("(g j c) -> j g c", g=3, j=J)).then_inc(d_bias, 16)
            act.dma_start(bhh[:, :, :], b_hh.rearrange("(g j c) -> j g c", g=3, j=J)).then_inc(d_bias, 16)
            for a in range(A):
                act.dma_start(Whh[:, a, :], rows_T(w_hh)[a]).then_inc(d_whh, 16)
            for s, (part, count) in enumerate(((bhi, 5), (bmid, 7), (blow, 8))):
                act.wait_ge(c_bias, count)
                act.dma_start(bias3[J * s:J * s + J, :, :], part[:, :, :]).then_inc(d_bias3, 16)
            act.wait_ge(c_warm, 1)
            act.activation(r_sb[:, :], warm[:, 0:C], ACT.Sigmoid).then_inc(a_first, 1)
            act.wait_ge(a_first, 1)

            def sum_squares(t):
                act.wait_ge(v_x1, t + 1)
                if t >= 2:
                    act.wait_ge(a_ss, t - 1)
                act.activation(sq_junk[:, t % 2, :], X1[:, t, :], ACT.Square, accum_out=ssq[:, t:t + 1]).then_inc(a_ss, 1)

            for t in range(T):
                act.wait_ge(p_r, t + 1)
                if t >= 1:
                    act.wait_ge(v_rh, t)
                act.activation(r_sb[:, :], psR[t % 2], ACT.Sigmoid).then_inc(a_r, 1)
                act.wait_ge(p_Z, t + 1)
                if t >= 1:
                    act.wait_ge(v_u, t)
                act.activation(z_sb[:, :], psZ[t % 2], ACT.Sigmoid).then_inc(a_z, 1)
                act.wait_ge(v_npre, t + 1)
                if t >= 1:
                    act.wait_ge(v_u, t)
                act.activation(n_sb[:, :], npre, ACT.Tanh).then_inc(a_n, 1)
                if t >= 1:
                    sum_squares(t - 1)
            sum_squares(T - 1)
            act.wait_ge(v_yT, T)
            act.activation(y_hi[:, :, :, T - G:T], yT[:, :, :, T - G:T], ACT.Copy).then_inc(a_yhi, 1)

            def squares(n):
                act.wait_ge(p_qk, n + 1)
                if n >= 1:
                    act.wait_ge(v_ss, n)
                act.activation(sq[:, :], psQK[n % 3], ACT.Square).then_inc(a_sq, 1)

            def roots(k):
                act.wait_ge(v_inv, k + 1)
                act.activation(qkr[:, batch(k), :], qkinv[:, batch(k), :], ACT.Sqrt).then_inc(a_rr, 1)

            def v_operand(n):
                act.wait_ge(p_v, n + 1)
                act.wait_ge(c_v, 2 * n + 2)
                for b in range(BT):
                    rows = slice(32 * b, 32 * b + 32)
                    act.activation(vblk[rows, n, :, DH * b:DH * b + DH],
                                   psV[n % 2][rows, 0:D].rearrange("p (h d) -> p h d", d=DH), ACT.Copy).then_inc(a_v, 1)

            def k_T(n):
                act.wait_ge(c_gk, 2)
                act.wait_ge(p_t, n + 1)
                if n >= 2:
                    act.wait_ge(p_s, n - 1)
                for s in range(4):
                    act.activation(k4[:, n % 2, :, s, :], psT[n % 2][:, 2 * P:4 * P].rearrange("p (a t) -> p a t", a=A),
                                   ACT.Copy, scale=row_mask[:, s:s + 1]).then_inc(a_k, 1)

            def q_T(n):
                act.activation(qT[:, n % 2, :, :], psT[n % 2][:, 0:2 * P].rearrange("p (a t) -> p a t", a=A), ACT.Copy,
                               scale=gq_p[:, 0:1]).then_inc(a_q, 1)

            def exps(n):
                act.wait_ge(v_sm, n + 1)
                if n >= 1:
                    act.wait_ge(v_pT, n)
                act.activation(ex[:, :], sm[:, n % 2, :, :, :].rearrange("p g c k -> p (g c k)"), ACT.Exp).then_inc(a_e, 1)

            def y_copy(n):
                act.wait_ge(p_y, n + 1)
                if n >= 2:
                    act.wait_ge(g_fin, n - 1)
                act.activation(y_out[:, n % 2, :], psY[:, 0:D], ACT.Copy).then_inc(a_y, 1)

            for n in range(NT):
                squares(n)
                if n >= 1:
                    v_operand(n - 1)
                if n == NB:
                    roots(0)
                if n == NT - 2:
                    k_T(0)
                    q_T(0)
            v_operand(NT - 1)
            k_T(1)
            q_T(1)
            roots(1)
            act.activation(ex[:, 0:1], qkr[:, 0, 0:1], ACT.Exp).then_inc(a_exp_in, 1)
            act.wait_ge(a_exp_in, 1)
            exps(0)
            for i in turns:
                if due(i, LAG_S) and i > LAG_S:
                    exps(i - LAG_S)
                if due(i, LAG_Y) and i - LAG_Y < NT - 1:
                    y_copy(i - LAG_Y)
                if 1 <= i < NT - 1:
                    k_T(i + 1)
                    q_T(i + 1)

        @block.vector
        def _(dve):
            dve.memset(warm[:, :], 0.0).then_inc(c_warm, 1)
            dve.wait_ge(d_bias, 32)
            dve.tensor_tensor(bsum[:, 0, :], bih[:, 0, :], bhh[:, 0, :], ALU.add).then_inc(c_bias, 1)
            dve.tensor_tensor(bsum[:, 3, :], bih[:, 1, :], bhh[:, 1, :], ALU.add).then_inc(c_bias, 1)
            dve.tensor_copy(bsum[:, 1, :], bhh[:, 2, :]).then_inc(c_bias, 1)
            dve.tensor_copy(bsum[:, 2, :], bih[:, 2, :]).then_inc(c_bias, 1)
            dve.wait_ge(c_bias, 4)
            dve.tensor_copy(bhi[:, :, :], bsum[:, :, :]).then_inc(c_bias, 1)
            dve.wait_ge(c_bias, 5)
            dve.tensor_tensor(blo[:, :, :], bsum[:, :, :], bhi[:, :, :], ALU.subtract).then_inc(c_bias, 1)
            dve.wait_ge(c_bias, 6)
            dve.tensor_copy(bmid[:, :, :], blo[:, :, :]).then_inc(c_bias, 1)
            dve.wait_ge(c_bias, 7)
            dve.tensor_tensor(blow[:, :, :], blo[:, :, :], bmid[:, :, :], ALU.subtract).then_inc(c_bias, 1)

            def part_of(t):
                return 0 if t < XCUT[1] else 1 if t < XCUT[2] else 2

            def x_transpose(t):
                dve.wait_ge(d_x[part_of(t)], 16 * (J if t >= XCUT[1] else XCUT[1]))
                if t >= 2:
                    dve.wait_ge(p_Z, t - 1)
                dve.transpose(xT[:, t % 2, :, :].rearrange("p a b -> p (a b)"), X[:, t, :]).then_inc(v_xT, 1)

            dve.wait_ge(d_cond, 16)
            dve.transpose(hT[:, 0, :, :].rearrange("p a b -> p (a b)"), H[:, 0, :]).then_inc(v_hT, 1)
            dve.transpose(condT[:, :, :].rearrange("p a b -> p (a b)"), H[:, 0, :]).then_inc(c_condT, 1)
            x_transpose(0)
            x_transpose(1)
            def residual(t):
                dve.wait_ge(v_h, t + 1)
                dve.tensor_tensor(X1[:, t, :], X[:, t, :], H[:, t + 1, :], ALU.add).then_inc(v_x1, 1)

            def mean_square(q):
                dve.wait_ge(p_ss, q + 1)
                dve.tensor_scalar(ms[:, G * q:G * q + G], psM[:, G * q:G * q + G], 1.0 / D, EPS,
                                  ALU.mult, ALU.add).then_inc(v_ms, 1)

            def norm(t):
                dve.wait_ge(g_rms, t // G + 1)
                dve.wait_ge(v_x1, t + 1)
                dve.wait_ge(v_gs, 3)
                dve.scalar_tensor_tensor(out=y0[:, 0, :], in0=X1[:, t, :], scalar=rms[:, t:t + 1], in1=gain[:, :],
                                         op0=ALU.mult, op1=ALU.mult).then_inc(v_y0, 1)
                dve.wait_ge(v_y0, t + 1)
                dve.tensor_tensor(y[:, 0, :], y0[:, 0, :], shift[:, :], ALU.add).then_inc(v_y, 1)
                dve.wait_ge(v_y, t + 1)
                dve.transpose(yT[:, :, :, t], y[:, 0, :]).then_inc(v_yT, 1)

            wide = [P, G, C]

            def scale_group(q):
                s, first = slice(G * q, G * q + G), G * q
                dve.wait_ge(g_rms, q + 1)
                dve.wait_ge(v_x1, first + G)
                dve.wait_ge(v_gs, 3)
                dve.wait_ge(v_yT, first)
                dve.tensor_tensor(y0[:, :, :], X1[:, s, :], rms[:, s].unsqueeze(2).broadcast_to(wide), ALU.mult).then_inc(v_y0, 1)

            def norm_group(q):
                first = G * q
                dve.wait_ge(v_y0, first + 1)
                dve.tensor_tensor(y[:, :, :], y0[:, :, :], gain[:, :].unsqueeze(1).broadcast_to(wide), ALU.mult).then_inc(v_y, G)
                dve.wait_ge(v_y, first + G)
                dve.tensor_tensor(y0[:, :, :], y[:, :, :], shift[:, :].unsqueeze(1).broadcast_to(wide), ALU.add).then_inc(v_y0, G - 1)
                dve.wait_ge(v_y0, first + G)
                for k in range(G):
                    dve.transpose(yT[:, :, :, first + k], y0[:, k, :]).then_inc(v_yT, 1)

            def conditioning():
                dve.wait_ge(d_emb, 16 * (A + 3))
                dve.wait_ge(p_E, 1)
                dve.scalar_tensor_tensor(out=gain[:, :], in0=psE[:, 0:C], scalar=1.0, in1=bemb_jb[:, 0, :],
                                         op0=ALU.add, op1=ALU.add).then_inc(v_gs, 1)
                dve.tensor_tensor(shift[:, :], psE[:, C:2 * C], bemb_jb[:, 1, :], ALU.add).then_inc(v_gs, 1)
                dve.wait_ge(v_gs, 1)
                dve.tensor_tensor(gain[:, :], gain[:, :], gnorm_jb[:, :], ALU.mult).then_inc(v_gs, 1)

            LAG = G + 2
            for t in range(T):
                h_new = H[:, t + 1, :]
                dve.wait_ge(p_hn, t + 1)
                dve.wait_ge(a_r, t + 1)
                dve.tensor_tensor(rh[:, :], psN[t % 2][:, 0:C], r_sb[:, :], ALU.mult).then_inc(v_rh, 1)
                dve.wait_ge(v_rh, t + 1)
                dve.tensor_tensor(npre, psN[t % 2][:, C:2 * C], rh[:, :], ALU.add).then_inc(v_npre, 1)
                dve.wait_ge(a_z, t + 1)
                dve.tensor_tensor(zh[:, :], z_sb[:, :], H[:, t, :], ALU.mult).then_inc(v_zh, 1)
                dve.wait_ge(a_n, t + 1)
                dve.scalar_tensor_tensor(out=u_sb[:, :], in0=z_sb[:, :], scalar=1.0, in1=n_sb[:, :],
                                         op0=ALU.subtract, op1=ALU.mult).then_inc(v_u, 1)
                dve.wait_ge(v_u, t + 1)
                dve.tensor_tensor(h_new, zh[:, :], u_sb[:, :], ALU.subtract).then_inc(v_h, 1)
                dve.wait_ge(v_h, t + 1)
                if t < T - 1:
                    dve.transpose(hT[:, (t + 1) % 2, :, :].rearrange("p a b -> p (a b)"), h_new).then_inc(v_hT, 1)
                residual(t)
                if t + 2 < T:
                    x_transpose(t + 2)
                if t == EMB_STEP:
                    conditioning()
                if t % G == 1 and t > G:
                    mean_square(t // G - 1)
                if t >= LAG + 1 and t - LAG - 1 < T - 2 * G:
                    norm(t - LAG - 1)
            scale_group(T // G - 2)
            mean_square(T // G - 1)
            norm_group(T // G - 2)
            scale_group(T // G - 1)
            norm_group(T // G - 1)
            dve.wait_ge(a_yhi, 1)
            dve.tensor_tensor(y_lo[:, :, :, T - G:T], yT[:, :, :, T - G:T], y_hi[:, :, :, T - G:T], ALU.subtract).then_inc(v_ylo, 1)

            dve.wait_ge(d_gqk, 16 * 2)
            dve.wait_ge(c_mask, 3)
            dve.wait_ge(c_ident, 2)
            dve.tensor_scalar(gq_p[:, :], gq_p[:, :], DH ** -0.5, None, ALU.mult).then_inc(c_gk, 1)
            dve.tensor_reduce(row_mask[:, :], head_rows[:, :, :].rearrange("p g s -> p s g"), AX.X, ALU.add).then_inc(c_half, 1)
            dve.wait_ge(c_half, 1)
            dve.tensor_scalar(row_mask[:, :], row_mask[:, :], gk_p[:, 0:1], None, ALU.mult).then_inc(c_gk, 1)
            dve.wait_ge(d_out_w, 16 * A)
            for a in range(A):
                dve.tensor_tensor(Wout[:, a, P * a:P * a + P], Wout[:, a, P * a:P * a + P], ident[:, :],
                                  ALU.add).then_inc(c_wout, 1)

            def qk_sums(n):
                dve.wait_ge(a_sq, n + 1)
                dve.tensor_reduce(qkss[:, n, :], sq[:, :].rearrange("p (h d) -> p h d", d=DH), AX.X, ALU.add).then_inc(v_ss, 1)

            def qk_copy(n):
                dve.wait_ge(a_sq, n + 1)
                dve.tensor_copy(qk[:, n, :], psQK[n % 3]).then_inc(v_qk, 1)

            def inverses(k):
                dve.wait_ge(v_ss, NB * k + NB)
                dve.tensor_scalar(qkms[:, batch(k), :], qkss[:, batch(k), :], 1.0 / DH, EPS, ALU.mult, ALU.add).then_inc(v_ms2, 1)
                dve.wait_ge(v_ms2, k + 1)
                dve.reciprocal(qkinv[:, batch(k), :], qkms[:, batch(k), :]).then_inc(v_inv, 1)

            def softmax_shift(n):
                S = psS[:, n % 2, :, 0:8 * T].rearrange("p g (c k) -> p g c k", k=T)
                dve.wait_ge(p_s, n + 1)
                if n >= 2:
                    dve.wait_ge(v_sm, n - 1)
                dve.tensor_reduce(mx[:, n % 2, :, :], S, AX.X, ALU.max).then_inc(v_mx, 1)
                dve.wait_ge(v_mx, n + 1)
                if n >= 2:
                    dve.wait_ge(a_e, n - 1)
                dve.tensor_tensor(sm[:, n % 2, :, :, :], S, mx[:, n % 2, :, :].unsqueeze(3).broadcast_to([P, 2, 8, T]),
                                  ALU.subtract).then_inc(v_sm, 1)

            def p_transpose(n):
                dve.wait_ge(a_e, n + 1)
                if n >= 2:
                    dve.wait_ge(p_o, n - 1)
                dve.transpose(pT[:, n % 2, :], ex[:, :]).then_inc(v_pT, 1)

            def o_norm(n):
                O = psO[:, 0:4 * VW].rearrange("p (c w) -> p c w", w=VW)
                dve.wait_ge(p_o, n + 1)
                dve.reciprocal(rden[:, :, :], O[:, :, BT * DH:VW]).then_inc(v_rd, 1)
                dve.wait_ge(v_rd, n + 1)
                dve.tensor_tensor(o_n[:, :, :, :].rearrange("p b c d -> p c b d"),
                                  O[:, :, 0:BT * DH].rearrange("p c (b d) -> p c b d", d=DH),
                                  rden[:, :, :].unsqueeze(3).broadcast_to([P, 4, BT, DH]), ALU.mult).then_inc(v_on, 1)
                dve.wait_ge(v_on, n + 1)
                if n >= 2:
                    dve.wait_ge(p_y, n - 1)
                for a in range(A):
                    dve.transpose(oT[:, n % 2, a, :, :],
                                  o_n[:, :, 2 * a:2 * a + 2, :].rearrange("p b s d -> p b (s d)")).then_inc(v_oT, 1)

            def last_tile_residual():
                n = NT - 1
                dve.wait_ge(p_y, n + 1)
                dve.wait_ge(d_x1ld, 16)
                dve.wait_ge(d_res[n % 2], 16 * (n // 2))
                dve.tensor_tensor(fin[:, n % 2, :], psY[:, 0:D], x1tok[:, n, :], ALU.add).then_inc(v_fin, 1)

            for n in range(NT):
                qk_sums(n)
                if n < NT - 1:
                    qk_copy(n)
                if n % NB == NB - 1:
                    inverses(n // NB)
            qk_copy(NT - 1)
            for i in turns:
                if due(i, LAG_P):
                    p_transpose(i - LAG_P)
                if due(i, LAG_S):
                    softmax_shift(i - LAG_S)
                if due(i, LAG_P):
                    o_norm(i - LAG_P)
            last_tile_residual()

        @block.tensor
        def _(pe):
            wih = Wih[:, :, :].rearrange("p a (g n) -> p a g n", g=3)
            whh = Whh[:, :, :].rearrange("p a (g n) -> p a g n", g=3)
            wemb = Wemb[:, :, :].rearrange("p a (g n) -> p a g n", g=2)

            def by_gate(ps):
                return ps.rearrange("p (g c) -> p g c", c=C)

            def tiles(ps, stationary, moving, start, stop):
                for j in range(J):
                    last = pe.matmul(ps[32 * j:32 * j + 32, :, :], stationary, moving[:, :, C * j:C * j + C],
                                     start=start, stop=stop, skip_group_check=True)
                return last

            def x_gates(t):
                pr, pn, pz = by_gate(psR[t % 2]), by_gate(psN[t % 2]), by_gate(psZ[t % 2])
                if t >= 2:
                    pe.wait_ge(a_z, t - 1)
                    pe.wait_ge(v_npre, t - 1)
                for ps, gates in ((pr, slice(0, 1)), (pn, slice(1, 3)), (pz, slice(3, 4))):
                    pe.matmul(ps, to_jb[:, :], bias3[:, gates, :], start=True, stop=False, skip_group_check=True)
                pe.wait_ge(v_xT, t + 1)
                for ps, gate in ((pr, 0), (pn[:, 1:2, :], 2), (pz, 1)):
                    for a in range(A):
                        tiles(ps, xT[:, t % 2, a, :], wih[:, a, gate:gate + 1, :], False, False)

            def h_gates(t):
                pr, pn, pz = by_gate(psR[t % 2]), by_gate(psN[t % 2]), by_gate(psZ[t % 2])
                pe.wait_ge(v_hT, t + 1)
                for ps, gate, done in ((pr, 0, p_r), (pn[:, 0:1, :], 2, p_hn), (pz, 1, p_Z)):
                    for a in range(A):
                        last = tiles(ps, hT[:, t % 2, a, :], whh[:, a, gate:gate + 1, :], False, a == A - 1)
                    last.then_inc(done, 1)

            def keep_open(k, bank):
                for _ in range(k):
                    pe.matmul(bank[:, 0:2 * P], warm[:, 0:P], warm[:, 0:2 * P], start=True, stop=True, skip_group_check=True)

            pe.wait_ge(c_warm, 1)
            for k in range(WARM):
                pe.matmul(banks[3], warm[:, 0:P], warm[:, :], start=True, stop=True, skip_group_check=True)
            pe.wait_ge(c_to_jb, 5)
            pe.wait_ge(d_bias3, 16 * 3)
            pe.wait_ge(d_wih, 16 * A)
            x_gates(0)
            pe.wait_ge(d_whh, 16 * A)
            for t in range(T):
                h_gates(t)
                if t == EMB_STEP:
                    pe.wait_ge(c_condT, 1)
                    pe.wait_ge(d_emb, 16 * (A + 3))
                    for a in range(A):
                        last = tiles(by_gate(psE), condT[:, a, :], wemb[:, a, :, :], a == 0, a == A - 1)
                    last.then_inc(p_E, 1)
                if t + 1 < T:
                    x_gates(t + 1)
                if t % G == 0 and t > 0:
                    q = t // G - 1
                    if q == 0:
                        pe.wait_ge(c_same, 1 + J)
                        pe.wait_ge(v_gs, 2)
                    pe.wait_ge(a_ss, G * q + G)
                    if q >= 1:
                        pe.wait_ge(v_ms, q)
                    pe.matmul(psM[:, G * q:G * q + G], same_b[:, :], ssq[:, G * q:G * q + G],
                              start=True, stop=True, skip_group_check=True).then_inc(p_ss, 1)
            keep_open(WARM_END, psY)
            q = T // G - 1
            pe.wait_ge(a_ss, T)
            pe.wait_ge(v_ms, q)
            pe.matmul(psM[:, G * q:G * q + G], same_b[:, :], ssq[:, G * q:G * q + G],
                      start=True, stop=True, skip_group_check=True).then_inc(p_ss, 1)

            keep_open(WARM_NORM, psY)

            def three_products(ps, n, cols):
                parts = [(y_hi, w_hi), (y_hi, w_lo), (y_lo, w_hi)]
                for k, (y_part, w_part) in enumerate(parts):
                    for a in range(A):
                        toks = y_part[:, a, BT * n:BT * n + BT, :].rearrange("p b t -> p (b t)")
                        last = pe.matmul(ps, toks, w_part[:, a, cols], start=(k == 0 and a == 0),
                                         stop=(k == len(parts) - 1 and a == A - 1))
                return last

            def project(n):
                if n == 0:
                    pe.wait_ge(g_wlo, A)
                    pe.wait_ge(g_ylo, T // G - 1)
                    pe.wait_ge(a_yhi, 1)
                    pe.wait_ge(v_ylo, 1)
                if n >= 3:
                    pe.wait_ge(v_qk, n - 2)
                three_products(psQK[n % 3], n, slice(0, 2 * D)).then_inc(p_qk, 1)

            def project_v(n):
                if n >= 2:
                    pe.wait_ge(a_v, BT * (n - 1))
                three_products(psV[n % 2][:, 0:D], n, slice(2 * D, 3 * D)).then_inc(p_v, 1)

            def transposes(n):
                pe.wait_ge(g_qkn, n + 1)
                if n >= 2:
                    pe.wait_ge(a_q, n - 1)
                for c in range(4):
                    last = pe.transpose(psT[n % 2][:, P * c:P * c + P], qkn[:, n % 2, P * c:P * c + P], ident[:, :])
                last.then_inc(p_t, 1)

            def scores(n):
                pe.wait_ge(a_q, n + 1)
                pe.wait_ge(a_k, 4 * n + 4)
                if n == 0:
                    pe.wait_ge(v_qk, NT - 2)
                if n == 1:
                    pe.wait_ge(a_v, BT * NT)
                if n >= 2:
                    pe.wait_ge(v_sm, n - 1)
                for a in range(A):
                    for b in range(BT):
                        cols = slice(32 * b, 32 * b + 32)
                        for g in range(2):
                            rows = slice(64 * g, 64 * g + 64)
                            last = pe.matmul(psS[cols, n % 2, g, 4 * T * a:4 * T * a + 4 * T].rearrange("p (s k) -> p s k", k=T),
                                             qT[rows, n % 2, a, cols], k4[rows, n % 2, a, :, cols], start=True, stop=True)
                last.then_inc(p_s, 1)

            def attend(n):
                pe.wait_ge(v_pT, n + 1)
                pe.wait_ge(a_v, BT * (n + 1))
                if n >= 1:
                    pe.wait_ge(v_on, n)
                for cs in range(4):
                    for g in range(4):
                        h = 8 * (cs // 2) + 2 * g + cs % 2
                        col = 8 * (g // 2) + 4 * (cs // 2) + h % 4
                        last = pe.matmul(psO[32 * g:32 * g + 32, VW * cs:VW * cs + VW], pT[:, n % 2, T * col:T * col + T],
                                         vblk[:, n, h, :], start=True, stop=True)
                last.then_inc(p_o, 1)

            def out_project(n):
                pe.wait_ge(v_oT, A * (n + 1))
                pe.wait_ge(c_wout, A)
                if n >= 1:
                    pe.wait_ge(a_y, n)
                for a in range(A):
                    last = pe.matmul(psY[:, 0:D], oT[:, n % 2, a, :, :].rearrange("p b t -> p (b t)"), Wout[:, a, :],
                                     start=(a == 0), stop=(a == A - 1))
                last.then_inc(p_y, 1)

            pe.wait_ge(c_ident, 2)
            for n in range(NT):
                project(n)
                if n >= 1:
                    project_v(n - 1)
                if n == NT - 2:
                    transposes(0)
            project_v(NT - 1)
            transposes(1)
            pe.wait_ge(v_qk, NT - 1)
            keep_open(FILL_0, psO)
            for i in turns:
                if due(i, LAG_S):
                    scores(i - LAG_S)
                if 1 <= i < FILL_TURNS:
                    keep_open(FILL, psO)
                if 1 <= i < NT - 1:
                    transposes(i + 1)
                if due(i, LAG_P):
                    attend(i - LAG_P)
                if due(i, LAG_Y):
                    out_project(i - LAG_Y)


_INS = ["x", "cond_2048", "L0_cond_W_ih", "L0_cond_W_hh", "L0_cond_b_ih", "L0_cond_b_hh", "L1_cond_W_emb",
        "L1_cond_b_emb", "L1_cond_g_norm", "L1_cond_W_qkv", "L1_cond_g_q", "L1_cond_g_k", "L1_cond_W_out"]


def kernel(**inputs):
    import numpy as _np
    import concourse.bacc as _bacc
    from concourse import mybir as _mybir
    from concourse.bass_utils import run_bass_kernel_spmd as _run

    nc = _bacc.Bacc("TRN2", target_bir_lowering=False, num_devices=1)
    arrays, args = {}, []
    for name in _INS:
        a = _np.ascontiguousarray(inputs[name])
        arrays[f"in_{name}_dram"] = a
        args.append(nc.dram_tensor(f"in_{name}_dram", a.shape, _mybir.dt.from_np(a.dtype), kind="ExternalInput").ap())
    args.append(nc.dram_tensor("out_0_dram", (B, T, D), F32, kind="ExternalOutput").ap())
    args.append(nc.dram_tensor("x1_scratch", (B, T, D), F32, kind="Internal").ap())
    build(nc, *args)
    r = _run(nc, [arrays], core_ids=[0])
    return r.results[0]["out_0_dram"]
```
